# Optimizing a Trainium2 kernel written in Bass

```python
import numpy as np
import jax
import jax.numpy as jnp

def _softmax(x, axis=-1):
    return jax.nn.softmax(x, axis=axis)

def _gelu(x):
    return jax.nn.gelu(x, approximate=True)

def _silu(x):
    return jax.nn.silu(x)

def _sigmoid(x):
    return jax.nn.sigmoid(x)

def _layernorm(x, axis=-1, eps=1e-05):
    m = jnp.mean(x, axis=axis, keepdims=True)
    v = jnp.var(x, axis=axis, keepdims=True)
    return (x - m) / jnp.sqrt(v + eps)

def _scatter_add(tgt, idx, src, axis=0):
    return tgt.at[idx].add(src)

def _segment_sum(src, seg, n):
    return jax.ops.segment_sum(src, seg, n)
kernel_name = 'mk_seq_preln_d1_jaxref_r8_043018'

def setup_inputs(seed: int=0):
    np.random.seed(seed)
    _w = jnp.asarray

    def _L0_attn_setup():
        import jax, jax.numpy as jnp
        import numpy as np
        import math
        B, L, D, H = (32, 64, 512, 32)
        HD = D // H
        key = jax.random.key(seed)
        ks = jax.random.split(key, 9)
        s = 1.0 / math.sqrt(D)
        return {'x': jax.random.normal(ks[0], (B, L, D), jnp.float32), 'Wq': jax.random.normal(ks[1], (D, D), jnp.float32) * s, 'bq': jax.random.normal(ks[2], (D,), jnp.float32) * s, 'Wk': jax.random.normal(ks[3], (D, D), jnp.float32) * s, 'bk': jax.random.normal(ks[4], (D,), jnp.float32) * s, 'Wv': jax.random.normal(ks[5], (D, D), jnp.float32) * s, 'bv': jax.random.normal(ks[6], (D,), jnp.float32) * s, 'Wo': jax.random.normal(ks[7], (D, D), jnp.float32) * s, 'bo': jax.random.normal(ks[8], (D,), jnp.float32) * s}
    _L0_attn_in = _L0_attn_setup()

    def _L0_ffn_setup():
        import jax, jax.numpy as jnp
        import numpy as np
        B_, S, D = (4, 512, 512)
        E, R, O = (8, 16, 512)
        TOP_K = 2
        SCALING = 8.0 / R
        key = jax.random.key(seed)
        ks = jax.random.split(key, 5)
        x = jax.random.normal(ks[0], (B_, S, D), dtype=jnp.float32)
        router_w = jax.random.normal(ks[1], (E, D), dtype=jnp.float32) * (1.0 / np.sqrt(D))
        router_b = jax.random.normal(ks[2], (E,), dtype=jnp.float32) * 0.01
        A = jax.random.normal(ks[3], (E, R, D), dtype=jnp.float32) * (1.0 / np.sqrt(D))
        Bm = jax.random.normal(ks[4], (E, O, R), dtype=jnp.float32) * 0.02
        return {'x': x, 'router_w': router_w, 'router_b': router_b, 'A': A, 'Bm': Bm}
    _L0_ffn_in = _L0_ffn_setup()
    _d = {'L0_attn_x': _L0_attn_in['x'], 'L0_attn_Wq': _L0_attn_in['Wq'], 'L0_attn_bq': _L0_attn_in['bq'], 'L0_attn_Wk': _L0_attn_in['Wk'], 'L0_attn_bk': _L0_attn_in['bk'], 'L0_attn_Wv': _L0_attn_in['Wv'], 'L0_attn_bv': _L0_attn_in['bv'], 'L0_attn_Wo': _L0_attn_in['Wo'], 'L0_attn_bo': _L0_attn_in['bo'], 'L0_ffn_router_w': _L0_ffn_in['router_w'], 'L0_ffn_router_b': _L0_ffn_in['router_b'], 'L0_ffn_A': _L0_ffn_in['A'], 'L0_ffn_Bm': _L0_ffn_in['Bm']}
    _x0 = _d['L0_attn_x']
    _d['L0_attn_x'] = jax.random.normal(jax.random.fold_in(jax.random.key(seed), 1), (2, 1024, 512), dtype=_x0.dtype)
    del _x0
    return _d

def reference(L0_attn_x, L0_attn_Wq, L0_attn_bq, L0_attn_Wk, L0_attn_bk, L0_attn_Wv, L0_attn_bv, L0_attn_Wo, L0_attn_bo, L0_ffn_router_w, L0_ffn_router_b, L0_ffn_A, L0_ffn_Bm):

    def _L0_attn_ref(x, Wq, bq, Wk, bk, Wv, bv, Wo, bo):
        import jax, jax.numpy as jnp
        import numpy as np
        import math
        B, L, D, H = (32, 64, 512, 32)
        HD = D // H
        b, l, d = x.shape
        h, hd = (H, HD)
        q = (x @ Wq.T + bq).reshape(b, l, h, hd).transpose(0, 2, 1, 3)
        k = (x @ Wk.T + bk).reshape(b, l, h, hd).transpose(0, 2, 1, 3)
        v = (x @ Wv.T + bv).reshape(b, l, h, hd).transpose(0, 2, 1, 3)
        scores = jnp.einsum('bhqd,bhkd->bhqk', q, k) / math.sqrt(hd)
        causal = jnp.tril(jnp.ones((l, l), bool))
        scores = jnp.where(causal, scores, -jnp.inf)
        att = jax.nn.softmax(scores, axis=-1)
        out = jnp.einsum('bhqk,bhkd->bhqd', att, v)
        out = out.transpose(0, 2, 1, 3).reshape(b, l, d)
        return out @ Wo.T + bo

    def _L0_ffn_ref(x, router_w, router_b, A, Bm):
        import jax, jax.numpy as jnp
        import numpy as np
        B_, S, D = (4, 512, 512)
        E, R, O = (8, 16, 512)
        TOP_K = 2
        SCALING = 8.0 / R
        flat = x.reshape(-1, x.shape[-1])
        N = flat.shape[0]
        logits = flat @ router_w.T + router_b
        probs = jax.nn.softmax(logits, axis=-1)
        topv, topi = jax.lax.top_k(probs, TOP_K)
        gates = topv / jnp.sum(topv, axis=-1, keepdims=True)
        w = jnp.zeros((N, E), dtype=flat.dtype).at[jnp.arange(N)[:, None], topi].add(gates)
        h = jnp.einsum('nd,erd->ner', flat, A)
        hw = h * w[:, :, None]
        out = jnp.einsum('ner,eor->no', hw, Bm) * SCALING
        return out.reshape(*x.shape[:-1], O)
    x = L0_attn_x
    x = x + _L0_attn_ref(_layernorm(x, axis=-1), L0_attn_Wq, L0_attn_bq, L0_attn_Wk, L0_attn_bk, L0_attn_Wv, L0_attn_bv, L0_attn_Wo, L0_attn_bo)
    x = x + _L0_ffn_ref(_layernorm(x, axis=-1), L0_ffn_router_w, L0_ffn_router_b, L0_ffn_A, L0_ffn_Bm)
    return x

_drawn_inputs = setup_inputs


def setup_inputs(seed=0):
    import zlib

    import numpy as np

    out = dict(_drawn_inputs(seed))
    spreads = {}
    factors = {'L0_attn_bq': 8.0, 'L0_attn_bk': 8.0, 'L0_ffn_router_b': 8.0}
    for name, (base, spread) in spreads.items():
        noise = np.random.default_rng([zlib.crc32(name.encode()), seed]).standard_normal(out[name].shape)
        drawn = base * np.exp(spread * noise) if base else spread * noise
        out[name] = jnp.asarray(drawn.astype(out[name].dtype))
    for name, factor in factors.items():
        out[name] = (out[name] * factor).astype(out[name].dtype)
    return out
```

```python
from contextlib import ExitStack

import concourse.bass as bass
from concourse import mybir

ALU = mybir.AluOpType
ACT = mybir.ActivationFunctionType
AX = mybir.AxisListType
F32 = mybir.dt.float32
BF16 = mybir.dt.bfloat16

P = 128
BATCH, L, D = 2, 1024, 512
H, HD = 32, 16
E, R, TOP = 8, 16, 2
ER = E * R
LORA_SCALE = 8.0 / R
EPS = 1e-5
Q_SCALE = HD ** -0.5
TT = L // P
KC = D // P
HG = 4
NG = H // HG
CH = 512
NCH = L // CH
TPC = CH // P
SLOT = P // HG
NEG = -1e30
LOW = -3e38

PARTS = 3
Q_PART = (0, 0, 0, 1, 1, 2)
K_PART = (0, 1, 2, 0, 1, 0)
TERMS = HD * len(Q_PART)
MROWS = 2

STEPS = [(c, kb, CH - P * max(0, kb - TPC * c)) for c in range(NCH) for kb in range(TPC * (c + 1))]
NS = len(STEPS)
DIAG = [kb >= TPC * c for c, kb, _ in STEPS]
ND = sum(DIAG)
LAST = [max(s for s in range(NS) if STEPS[s][0] == c) for c in range(NCH)]
UNITS = []
for _i in range(TT):
    for _j in range(HG):
        for _c in range(_i // TPC):
            UNITS.append((_i, _j, _c * CH, CH, False))
        UNITS.append((_i, _j, (_i // TPC) * CH, P * (_i % TPC + 1), True))
NU = len(UNITS)
DIAG_UNITS = [v for v in range(NU) if UNITS[v][4]]
NSPLIT = 2 * KC * NCH
STACK_DMAS = 2 * len(Q_PART)
BODY = 3
LOOPS = (NG - 2) // BODY


UNIT_STEPS = 10


def unit_cuts():
    step_cost = [w + 128 for _, _, w in STEPS[:UNIT_STEPS]]
    unit_cost = [u[3] + 128 for u in UNITS]
    cuts, v = [0], 0
    for s in range(UNIT_STEPS):
        while v < NU and sum(unit_cost[:v + 1]) * sum(step_cost) <= sum(unit_cost) * sum(step_cost[:s + 1]):
            v += 1
        cuts.append(v)
    return cuts


CUTS = unit_cuts()
assert CUTS[-1] == NU


def units_of(s):
    return range(CUTS[s], CUTS[s + 1]) if s < UNIT_STEPS else range(0)


LAST_UNIT_STEP = UNIT_STEPS - 1
OT_PREV_STEP, OT_STEP, MT_STEP = 2, LAST[0] + 3, LAST_UNIT_STEP + 1
ROUTER_OPS = 22
RT_EXP = 3

ST_PAIRS = 2 * NS
XR = 4
JUNK = 2
PROJ_BANK, PROJ_BANKS = 2, 4
ST_BANK = 2
NPROJ = NSPLIT + TT
LAPS = [len(range(r, NG, BODY)) for r in range(BODY)]
POOL_CONSTS = 9
VEC_CONSTS = 3 + E


def split_unit(u):
    return u // (2 * NCH), u // NCH % 2, u % NCH


def block_kernel(nc, x, wq, bq, wk, bk, wv, bv, wo, bo, rw, rb, la, lb, out):
    parts = nc.dram_tensor("qk_parts", [BATCH, 2, PARTS, D, L], BF16).ap()
    with ExitStack() as ctx:
        def sb(name, shape, dt=F32):
            return ctx.enter_context(nc.sbuf_tensor(name, shape, dt))

        def sem(name):
            return ctx.enter_context(nc.semaphore(name))

        ident = sb("ident", [P, P])
        ident_b = sb("ident_b", [P, P], BF16)
        strip = sb("strip", [P, CH])
        w_sb = {n: sb(f"w{n}_sb", [P, KC, D]) for n in "qkvo"}
        la_sb = sb("la_sb", [P, KC, ER + E])
        lb_sb = sb("lb_sb", [P, D])
        bias_qk = sb("bias_qk", [P, 2, KC])
        bv_row = sb("bv_row", [P, D])
        bo_row = sb("bo_row", [P, D])
        rb_row = sb("rb_row", [P, E])
        rank = sb("rank", [P, TT, E])
        x_in = sb("x_in", [P, XR, D])
        ln_stat = sb("ln_stat", [P, 2, 6])
        ln_mv = sb("ln_mv", [P, 2, 2])
        ln_var = sb("ln_var", [P, 2])
        ln_rstd = sb("ln_rstd", [P, 2])
        minus_half = sb("minus_half", [P, 1])
        xh = sb("xh", [P, 2, D])
        xhT = sb("xhT", [P, KC, L])
        att = xhT[:, :, :].rearrange("p a b -> p (a b)").rearrange("p (t d) -> p t d", t=TT)
        qf = sb("qf", [P, 2, CH])
        rest = sb("rest", [P, 2, CH])
        split = sb("split", [P, 2, PARTS, CH], BF16)
        v_sb = sb("v_sb", [P, TT, D])
        x2 = v_sb
        vg = sb("vg", [P, BODY, TT, HG, SLOT])
        qs = sb("qs", [P, BODY, HG, L], BF16)
        ks = sb("ks", [P, BODY, HG, L], BF16)
        mx = sb("mx", [P, NCH, HG * TT])
        mf = sb("mf", [P, HG * TT])
        mb = sb("mb", [P, P], BF16)
        mt = sb("mt", [P, P], BF16)
        junk = sb("junk", [P, JUNK, CH], BF16)
        pt = sb("pt", [P, 2, HG, CH])
        oT = sb("oT", [P, NCH, CH])
        rden = sb("rden", [P, 2, HG * TPC])
        attT = sb("attT", [P, 2, KC, P])
        x2T = sb("x2T", [P, 2, KC, P])
        h_sb = sb("h_sb", [P, TT, ER + E])
        hw = sb("hw", [P, TT, ER])
        hwT = sb("hwT", [P, 2, TPC, P])
        rt = sb("rt", [P, 7, TT, E])
        rs = sb("rs", [P, 8, TT])

        banks = ctx.enter_context(nc.psum_tensor("banks", [P, 8, CH], F32))
        O_BANK, M_BANK = 6, 7
        misc_b = banks[:, M_BANK, :].bitcast(BF16)

        s_w = {n: sem(f"w_{n}_loaded") for n in "qkvo"}
        s_small = sem("small_loaded")
        s_x = [sem(f"x_loaded{i}") for i in range(XR)]
        s_parts = [sem(f"parts_written{k}") for k in range(4)]
        s_stack = [sem(f"stack_loaded{i}") for i in range(BODY)]
        s_mrow = sem("max_rows_loaded")
        s_y = sem("y_stored")
        s_pool = sem("pool_consts")
        s_vec = sem("vector_consts")
        s_bias = sem("bias_scaled")
        s_stat = sem("ln_stats")
        s_aggr = sem("ln_aggregated")
        s_var = sem("ln_var_ready")
        s_rstd = sem("ln_rstd_ready")
        s_xh = sem("normed")
        s_xT = sem("normed_transposed")
        s_xTc = sem("normed_T_copied")
        s_proj = sem("projected")
        s_qf = sem("q_copied")
        s_q1 = sem("part1_ready")
        s_r1 = sem("rest_ready")
        s_q2 = sem("part2_ready")
        s_q3 = sem("part3_ready")
        s_v = sem("v_copied")
        s_sm = sem("unit_scores")
        s_max = sem("unit_max")
        s_mf = sem("row_max")
        s_m1 = sem("row_max_part1")
        s_mb = sem("row_max_parts")
        s_mT = sem("row_max_transposed")
        s_mt = sem("row_max_T_copied")
        s_st = sem("scores_T")
        s_exp = sem("probs_T")
        s_mask = sem("probs_masked")
        s_vg = sem("v_group_copied")
        s_pv = sem("pv_done")
        s_ot = sem("out_T_copied")
        s_oT = sem("out_transposed")
        s_rd = sem("denominators_inverted")
        s_on = sem("out_normalised")
        s_aT = sem("att_transposed")
        s_aTc = sem("att_T_copied")
        s_xb = sem("x_plus_bias")
        s_wo = sem("att_projected")
        s_x2 = sem("x2_ready")
        s_h = sem("experts_down")
        s_hc = sem("h_copied")
        s_rt = sem("router_step")
        s_re = sem("router_exp")
        s_hw = sem("h_gated")
        s_hT = sem("hw_transposed")
        s_hTc = sem("hw_T_copied")
        s_up = sem("experts_up")
        s_out = sem("y_ready")

        SMALL = 16 * 8

        def group_loop(eng, b, group):
            group(b * NG, 0, 0, True, False)
            with eng.Fori(0, LOOPS) as k:
                for q in range(BODY):
                    g = k * BODY + (1 + q)
                    group(b * NG + g, g, (1 + q) % BODY, False, False)
            group(b * NG + (NG - 1), NG - 1, (NG - 1) % BODY, False, True)

        block = ctx.enter_context(nc.Block())

        @block.sync
        def _(sp):
            for n, w in zip("qkvo", (wq, wk, wv, wo)):
                if n == "k":
                    sp.dma_start(bias_qk[:, 0, :], bq).then_inc(s_small, 16)
                    sp.dma_start(bias_qk[:, 1, :], bk).then_inc(s_small, 16)
                sp.dma_start(w_sb[n][:, :, :], w.rearrange("(k p) n -> p k n", p=P)).then_inc(s_w[n], 16)
            for row, src in ((bv_row, bv), (bo_row, bo), (rb_row, rb)):
                n = src.shape[0]
                sp.dma_start(row[:, :], src.rearrange("(a n) -> a n", a=1).to_broadcast([P, n])).then_inc(s_small, 16)
            sp.dma_start(la_sb[:, :, 0:ER], la.rearrange("(k p) n -> p k n", p=P)).then_inc(s_small, 16)
            sp.dma_start(la_sb[:, :, ER:ER + E], rw.rearrange("(k p) n -> p k n", p=P)).then_inc(s_small, 16)
            sp.dma_start(lb_sb[:, :], lb).then_inc(s_small, 16)

            with sp.Fori(0, BATCH) as b:
                parts_b = parts[bass.ds(b, 1)]
                x_b, out_b = x[bass.ds(b, 1)], out[bass.ds(b, 1)]
                for i in range(TT):
                    if i >= XR:
                        sp.wait_ge(s_xh, b * (2 * TT) + (i - XR + 1))
                    sp.dma_start(x_in[:, i % XR, :], x_b[0, i * P:(i + 1) * P, :]).then_inc(s_x[i % XR], 16)

                def store_parts(u):
                    t, w, c = split_unit(u)
                    sp.wait_ge(s_q1, b * NSPLIT + u + 1)
                    sp.wait_ge(s_q3, b * NSPLIT + u + 1)
                    dst = parts_b[0, w, :, t * P:(t + 1) * P, c * CH:(c + 1) * CH].rearrange("s d l -> d s l")
                    sp.dma_start(dst, split[:, u % 2, :, :]).then_inc(s_parts[u % 4], 16)

                def load_stack(g, r):
                    for w, dst, order in ((0, qs, Q_PART), (1, ks, K_PART)):
                        for n, part in enumerate(order):
                            src = parts_b[0, w, part, bass.ds(g * (HG * HD), HG * HD), :]
                            sp.dma_start(dst[n * HD:(n + 1) * HD, r, :, :],
                                         src.rearrange("(j d) l -> d j l", j=HG)).then_inc(s_stack[r], 16)

                def load_max_rows(n, r):
                    sp.wait_ge(s_mt, n + 1)
                    for m in range(MROWS):
                        sp.dma_start(qs[TERMS + m:TERMS + m + 1, r, :, :].rearrange("p j l -> p (j l)"),
                                     mt[m * HG * TT:(m + 1) * HG * TT, :]).then_inc(s_mrow, 16)

                for u in range(NSPLIT):
                    store_parts(u)
                for t in range(KC):
                    for k in range(4):
                        sp.wait_ge(s_parts[k], b * (16 * NSPLIT // 4) + 16 * (t + 1))
                    sp.nop(nofuse=True)
                    for g in range(t * NG // KC, min(BODY, (t + 1) * NG // KC)):
                        load_stack(g, g)
                load_max_rows(b * NG, 0)

                for g in range(NG - BODY):
                    load_max_rows(b * NG + (g + 1), (g + 1) % BODY)
                    sp.wait_ge(s_st, b * (NG * ST_PAIRS) + (g + 1) * ST_PAIRS)
                    load_stack(g + BODY, g % BODY)
                for g in range(NG - BODY + 1, NG):
                    load_max_rows(b * NG + g, g % BODY)

                for i in range(TT):
                    if i >= XR:
                        sp.wait_ge(s_x2, b * TT + (i - XR + 1))
                    sp.dma_start(x_in[:, i % XR, :], x_b[0, i * P:(i + 1) * P, :]).then_inc(s_x[i % XR], 16)
                for i in range(TT):
                    sp.wait_ge(s_out, b * TT + (i + 1))
                    sp.dma_start(out_b[0, i * P:(i + 1) * P, :], x2[:, i, :]).then_inc(s_y, 16)
            sp.wait_ge(s_y, BATCH * TT * 16)

        @block.gpsimd
        def _(pool):
            pool.memset(ident[:, :], 0.0).then_inc(s_pool, 1)
            pool.memset(ident_b[:, :], 0.0).then_inc(s_pool, 1)
            pool.memset(strip[:, :], 0.0).then_inc(s_pool, 1)
            pool.memset(vg[:, :, :, :, :], 0.0).then_inc(s_pool, 1)
            pool.memset(minus_half[:, :], -0.5).then_inc(s_pool, 1)
            pool.wait_ge(s_pool, 5)
            for m in (ident, ident_b):
                pool.affine_select(out=m[:, :], in_=m[:, :], compare_op=ALU.not_equal, fill=1.0, base=0,
                                   pattern=[[-1, P]], channel_multiplier=1).then_inc(s_pool, 1)
            pool.affine_select(out=strip[:, CH - P:], in_=strip[:, CH - P:], compare_op=ALU.is_ge, fill=NEG, base=0,
                               pattern=[[-1, P]], channel_multiplier=1).then_inc(s_pool, 1)
            pool.memset(vg[:, :, :, :, HD:HD + 1], 1.0).then_inc(s_pool, 1)
            pool.wait_ge(s_pool, POOL_CONSTS)
            with pool.Fori(0, BATCH) as b:
                def copy_v(n, g, r):
                    pool.tensor_copy(vg[:, r, :, :, 0:HD],
                                     v_sb[:, :, bass.ds(g * (HG * HD), HG * HD)].rearrange("p t (j d) -> p t j d", j=HG)
                                     ).then_inc(s_vg, 1)

                def inverse_deviation(m):
                    pool.wait_ge(s_var, b * (2 * TT) + (m + 1))
                    pool.tensor_tensor(out=ln_rstd[:, m % 2:m % 2 + 1], in0=ln_var[:, m % 2:m % 2 + 1],
                                       in1=minus_half[:, :], op=ALU.pow).then_inc(s_rstd, 1)

                for i in range(TT):
                    inverse_deviation(i)
                pool.wait_ge(s_v, b * TT + TT)
                pool.nop(nofuse=True)
                copy_v(b * NG, 0, 0)

                def group(n, g, r, first, last):
                    d = 0
                    for s in range(NS):
                        if DIAG[s]:
                            pool.wait_ge(s_exp, n * ST_PAIRS + 2 * (s + 1))
                            pool.nop(nofuse=True)
                            blk = pt[:, s % 2, :, 0:P]
                            pool.affine_select(out=blk, in_=blk, compare_op=ALU.is_ge, fill=0.0, base=0,
                                               pattern=[[0, HG], [1, P]], channel_multiplier=-1).then_inc(s_mask, 1)
                            d += 1
                        if s == LAST[0] + 1 and not last:
                            copy_v(n + 1, g + 1, (r + 1) % BODY)

                group_loop(pool, b, group)

                for i in range(TT):
                    pool.wait_ge(s_x[i % XR], b * (16 * 2 * TT // XR) + 16 * (TT // XR + i // XR + 1))
                    pool.wait_ge(s_small, SMALL)
                    pool.tensor_tensor(out=x_in[:, i % XR, :], in0=x_in[:, i % XR, :], in1=bo_row[:, :],
                                       op=ALU.add).then_inc(s_xb, 1)
                    if i:
                        inverse_deviation(TT + i - 1)
                inverse_deviation(TT + TT - 1)

        @block.scalar
        def _(act):
            with act.Fori(0, BATCH) as b:
                for i in range(TT):
                    act.wait_ge(s_xT, b * (2 * TT) + (i + 1))
                    act.activation(xhT[:, :, i * P:(i + 1) * P], banks[:, i % 2, :].rearrange("p (k c) -> p k c", k=KC),
                                   ACT.Copy).then_inc(s_xTc, 1)
                for u in range(NSPLIT):
                    t, w, c = split_unit(u)
                    act.wait_ge(s_proj, b * NPROJ + (u + 1))
                    if u == 0:
                        act.wait_ge(s_bias, 1)
                    if u >= 2:
                        act.wait_ge(s_q3, b * NSPLIT + (u - 1))
                        act.wait_ge(s_parts[(u - 2) % 4], b * (16 * NSPLIT // 4) + 16 * ((u - 2) // 4 + 1))
                    src = banks[:, PROJ_BANK + u % PROJ_BANKS, :]
                    scale = Q_SCALE if w == 0 else 1.0
                    act.activation(qf[:, u % 2, :], src, ACT.Identity, bias=bias_qk[:, w, t:t + 1],
                                   scale=scale).then_inc(s_qf, 1)
                    act.activation(split[:, u % 2, 0, :], src, ACT.Identity, bias=bias_qk[:, w, t:t + 1],
                                   scale=scale).then_inc(s_q1, 1)

                def copy_out(n, c):
                    act.wait_ge(s_pv, n * NS + (LAST[c] + 1))
                    act.activation(oT[:, c, :], banks[:, O_BANK, :], ACT.Copy).then_inc(s_ot, 1)

                def group(n, g, r, first, last):
                    for s, (c, kb, w) in enumerate(STEPS):
                        for hp in range(2):
                            q = 2 * s + hp
                            act.wait_ge(s_st, n * ST_PAIRS + (q + 1))
                            if not (first and s < 2):
                                act.wait_ge(s_pv, n * NS + (s - 1))
                            act.activation(pt[:, s % 2, 2 * hp:2 * hp + 2, 0:w],
                                           banks[:, ST_BANK + 2 * (q % 2):ST_BANK + 2 * (q % 2) + 2, 0:w],
                                           ACT.Exp).then_inc(s_exp, 1)
                        if s == 0 and not first:
                            copy_out(n - 1, 1)
                        if s == LAST[0] + 1:
                            copy_out(n, 0)

                group_loop(act, b, group)
                copy_out(b * NG + (NG - 1), 1)

                for i in range(TT + 4):
                    if i < TT:
                        act.wait_ge(s_aT, b * TT + (i + 1))
                        if i >= 2:
                            act.wait_ge(s_wo, b * TT + (i - 1))
                        act.activation(attT[:, i % 2, :, :], banks[:, i % 2, :].rearrange("p (k c) -> p k c", k=KC),
                                       ACT.Copy).then_inc(s_aTc, 1)
                    if 0 <= i - 3 < TT:
                        a = i - 3
                        act.wait_ge(s_xT, b * (2 * TT) + (TT + a + 1))
                        if a >= 2:
                            act.wait_ge(s_h, b * TT + (a - 1))
                        act.activation(x2T[:, a % 2, :, :], banks[:, 4 + a % 2, :].rearrange("p (k c) -> p k c", k=KC),
                                       ACT.Copy).then_inc(s_xTc, 1)
                    if 0 <= i - 4 < TT:
                        a = i - 4
                        act.wait_ge(s_h, b * TT + (a + 1))
                        act.activation(h_sb[:, a, :], banks[:, 6 + a % 2, 0:ER + E], ACT.Copy).then_inc(s_hc, 1)
                act.wait_ge(s_rt, b * ROUTER_OPS + RT_EXP)
                act.activation(rt[:, 2, :, :], rt[:, 1, :, :], ACT.Exp).then_inc(s_re, 1)
                for q in range(TT // TPC):
                    act.wait_ge(s_hT, b * (TT // TPC) + (q + 1))
                    act.activation(hwT[:, q, :, :], banks[:, q, :].rearrange("p (t c) -> p t c", t=TPC),
                                   ACT.Copy).then_inc(s_hTc, 1)

        @block.vector
        def _(dve):
            dve.memset(mx[:, :, :], LOW).then_inc(s_vec, 1)
            dve.memset(mb[:, :], 0.0).then_inc(s_vec, 1)
            dve.memset(ks[TERMS:TERMS + MROWS, :, :, :], -1.0).then_inc(s_vec, 1)
            for e in range(E):
                dve.memset(rank[:, :, e:e + 1], float(E - e)).then_inc(s_vec, 1)
            dve.wait_ge(s_vec, VEC_CONSTS)
            dve.wait_ge(s_pool, POOL_CONSTS)
            dve.wait_ge(s_small, SMALL)
            dve.tensor_scalar(bias_qk[:, 0, :], bias_qk[:, 0, :], Q_SCALE, None, ALU.mult).then_inc(s_bias, 1)

            with dve.Fori(0, BATCH) as b:
                def moments(src, m):
                    k = m % 2
                    dve.bn_stats(ln_stat[:, k, :], src).then_inc(s_stat, 1)
                    dve.wait_ge(s_stat, b * (2 * TT) + (m + 1))
                    dve.nop(nofuse=True)
                    dve.bn_aggr(ln_mv[:, k, :], ln_stat[:, k, :]).then_inc(s_aggr, 1)
                    dve.wait_ge(s_aggr, b * (2 * TT) + (m + 1))
                    dve.tensor_scalar(ln_var[:, k:k + 1], ln_mv[:, k, 1:2], EPS, None, ALU.add).then_inc(s_var, 1)

                def normed(src, i, m):
                    k = m % 2
                    dve.wait_ge(s_rstd, b * (2 * TT) + (m + 1))
                    if i >= 2:
                        dve.wait_ge(s_xT, b * (2 * TT) + (m - 1))
                    dve.tensor_scalar(xh[:, k, :], src, ln_mv[:, k, 0:1], ln_rstd[:, k:k + 1],
                                      ALU.subtract, ALU.mult).then_inc(s_xh, 1)

                for i in range(TT + 1):
                    if i < TT:
                        dve.wait_ge(s_x[i % XR], b * (16 * 2 * TT // XR) + 16 * (i // XR + 1))
                        moments(x_in[:, i % XR, :], i)
                    if i:
                        normed(x_in[:, (i - 1) % XR, :], i - 1, i - 1)

                for u in range(NSPLIT):
                    k = u % 2
                    dve.wait_ge(s_qf, b * NSPLIT + (u + 1))
                    dve.wait_ge(s_q1, b * NSPLIT + (u + 1))
                    dve.tensor_tensor(out=rest[:, k, :], in0=qf[:, k, :], in1=split[:, k, 0, :],
                                      op=ALU.subtract).then_inc(s_r1, 1)
                    dve.wait_ge(s_r1, b * NSPLIT + (u + 1))
                    dve.tensor_copy(split[:, k, 1, :], rest[:, k, :]).then_inc(s_q2, 1)
                    dve.wait_ge(s_q2, b * NSPLIT + (u + 1))
                    dve.tensor_tensor(out=split[:, k, 2, :], in0=rest[:, k, :], in1=split[:, k, 1, :],
                                      op=ALU.subtract).then_inc(s_q3, 1)
                for i in range(TT):
                    dve.wait_ge(s_proj, b * NPROJ + (NSPLIT + i + 1))
                    dve.tensor_tensor(out=v_sb[:, i, :], in0=banks[:, PROJ_BANK + (NSPLIT + i) % PROJ_BANKS, :],
                                      in1=bv_row[:, :], op=ALU.add).then_inc(s_v, 1)

                def unit_max(n, v):
                    i, j, k0, w, diag = UNITS[v]
                    dst = mx[:, k0 // CH, j * TT + i:j * TT + i + 1]
                    dve.wait_ge(s_sm, n * NU + (v + 1))
                    if diag:
                        m = DIAG_UNITS.index(v)
                        if m >= JUNK:
                            dve.wait_ge(s_max, n * NU + (DIAG_UNITS[m - JUNK] + 1))
                        dve.nop(nofuse=True)
                        dve.tensor_tensor_reduce(junk[:, m % JUNK, 0:w], banks[:, v % 2, 0:w], strip[:, CH - w:CH],
                                                 1.0, LOW, ALU.add, ALU.max, dst).then_inc(s_max, 1)
                    else:
                        dve.tensor_reduce(dst, banks[:, v % 2, :], AX.X, ALU.max).then_inc(s_max, 1)

                def max_parts(n):
                    dve.wait_ge(s_max, n * NU + NU)
                    dve.tensor_tensor(out=mf[:, :], in0=mx[:, 0, :], in1=mx[:, 1, :], op=ALU.max).then_inc(s_mf, 1)
                    dve.wait_ge(s_mf, n + 1)
                    dve.tensor_copy(mb[:, 0:HG * TT], mf[:, :]).then_inc(s_m1, 1)
                    dve.wait_ge(s_m1, n + 1)
                    dve.tensor_tensor(out=mb[:, HG * TT:2 * HG * TT], in0=mf[:, :], in1=mb[:, 0:HG * TT],
                                      op=ALU.subtract).then_inc(s_mb, 1)

                def copy_max_rows(n):
                    dve.wait_ge(s_mT, n + 1)
                    dve.tensor_copy(mt[0:MROWS * HG * TT, :], misc_b[0:MROWS * HG * TT, 0:P]).then_inc(s_mt, 1)

                def normalise(n, g, c):
                    src = banks[:, M_BANK, :].rearrange("p (t j s) -> p t j s", t=TPC, j=HG)
                    den = rden[:, c, :].rearrange("p (t j) -> p t j", t=TPC)
                    dve.wait_ge(s_oT, n * NCH + (c + 1))
                    dve.reciprocal(den, src[:, :, :, HD]).then_inc(s_rd, 1)
                    dve.wait_ge(s_rd, n * NCH + (c + 1))
                    dst = att[:, c * TPC:(c + 1) * TPC, bass.ds(g * (HG * HD), HG * HD)]
                    dve.tensor_tensor(out=dst.rearrange("p t (j d) -> p t j d", j=HG), in0=src[:, :, :, 0:HD],
                                      in1=den.unsqueeze(3).to_broadcast([P, TPC, HG, HD]), op=ALU.mult).then_inc(s_on, 1)

                for v in range(NU):
                    unit_max(b * NG, v)
                max_parts(b * NG)
                copy_max_rows(b * NG)

                def group(n, g, r, first, last):
                    for s in range(NS):
                        if not last:
                            for v in units_of(s):
                                unit_max(n + 1, v)
                            if s == LAST_UNIT_STEP:
                                max_parts(n + 1)
                            if s == MT_STEP + 1:
                                copy_max_rows(n + 1)
                        if s == OT_PREV_STEP + 1 and not first:
                            normalise(n - 1, g - 1, 1)
                        if s == OT_STEP + 1:
                            normalise(n, g, 0)

                group_loop(dve, b, group)
                normalise(b * NG + (NG - 1), NG - 1, 1)

                for i in range(TT + 1):
                    if i < TT:
                        dve.wait_ge(s_wo, b * TT + (i + 1))
                        dve.wait_ge(s_xb, b * TT + (i + 1))
                        dve.tensor_tensor(out=x2[:, i, :], in0=banks[:, 2 + i % 2, :], in1=x_in[:, i % XR, :],
                                          op=ALU.add).then_inc(s_x2, 1)
                        dve.wait_ge(s_x2, b * TT + (i + 1))
                        moments(x2[:, i, :], TT + i)
                    if i:
                        normed(x2[:, i - 1, :], i - 1, TT + i - 1)

                steps = [0]

                def link(ins):
                    steps[0] += 1
                    ins.then_inc(s_rt, 1)
                    dve.wait_ge(s_rt, b * ROUTER_OPS + steps[0])

                def over_experts(x):
                    return x.unsqueeze(2).to_broadcast([P, TT, E])

                def each(out, a, b_, op):
                    link(dve.tensor_tensor(out=out, in0=a, in1=b_, op=op))

                def row(n):
                    return rs[:, n, :]

                logits, shifted, expd, probs, tmp, first_hot, second_hot = (rt[:, n, :, :] for n in range(7))
                big, z, rz, p1, f1, p2, f2, rg = (row(n) for n in range(8))
                dve.wait_ge(s_hc, b * TT + TT)
                each(logits, h_sb[:, :, ER:ER + E], rb_row[:, :].unsqueeze(1).to_broadcast([P, TT, E]), ALU.add)
                link(dve.tensor_reduce(big, logits, AX.X, ALU.max))
                each(shifted, logits, over_experts(big), ALU.subtract)
                assert steps[0] == RT_EXP
                dve.wait_ge(s_re, b + 1)
                link(dve.tensor_reduce(z, expd, AX.X, ALU.add))
                link(dve.reciprocal(rz, z))
                each(probs, expd, over_experts(rz), ALU.mult)

                def take_best(src, best, mark, hot):
                    link(dve.tensor_reduce(best, src, AX.X, ALU.max))
                    each(tmp, src, over_experts(best), ALU.is_equal)
                    each(tmp, tmp, rank[:, :, :], ALU.mult)
                    link(dve.tensor_reduce(mark, tmp, AX.X, ALU.max))
                    each(hot, tmp, over_experts(mark), ALU.is_equal)

                take_best(probs, p1, f1, first_hot)
                link(dve.scalar_tensor_tensor(out=shifted, in0=first_hot, scalar=-2.0, in1=probs, op0=ALU.mult, op1=ALU.add))
                take_best(shifted, p2, f2, second_hot)
                each(rg, p1, p2, ALU.add)
                link(dve.reciprocal(rg, rg))
                each(tmp, first_hot, second_hot, ALU.add)
                link(dve.scalar_tensor_tensor(out=tmp, in0=tmp, scalar=LORA_SCALE, in1=probs, op0=ALU.mult, op1=ALU.mult))
                each(logits, tmp, over_experts(rg), ALU.mult)
                assert steps[0] == ROUTER_OPS, steps
                for t in range(TT):
                    dve.tensor_tensor(out=hw[:, t, :].rearrange("p (e r) -> p e r", e=E),
                                      in0=h_sb[:, t, 0:ER].rearrange("p (e r) -> p e r", e=E),
                                      in1=logits[:, t, :].unsqueeze(2).to_broadcast([P, E, R]), op=ALU.mult).then_inc(s_hw, 1)
                for i in range(TT):
                    dve.wait_ge(s_up, b * TT + (i + 1))
                    dve.tensor_tensor(out=x2[:, i, :], in0=banks[:, 2 + i % 4, :], in1=x2[:, i, :],
                                      op=ALU.add).then_inc(s_out, 1)

        @block.tensor
        def _(pe):
            pe.wait_ge(s_pool, POOL_CONSTS)
            with pe.Fori(0, BATCH) as b:
                def transpose_tile(bank, src, s):
                    for k in range(KC):
                        m = pe.transpose(banks[:, bank, k * P:(k + 1) * P], src[:, k * P:(k + 1) * P], ident[:, :])
                    m.then_inc(s, 1)

                for i in range(TT):
                    pe.wait_ge(s_xh, b * (2 * TT) + (i + 1))
                    if i >= 2:
                        pe.wait_ge(s_xTc, b * (2 * TT) + (i - 1))
                    transpose_tile(i % 2, xh[:, i % 2, :], s_xT)

                def bank_free(u):
                    v = u - PROJ_BANKS
                    if v >= NSPLIT:
                        pe.wait_ge(s_v, b * TT + (v - NSPLIT + 1))
                    elif v >= 0:
                        pe.wait_ge(s_q1, b * NSPLIT + (v + 1))

                for u in range(NSPLIT):
                    t, w, c = split_unit(u)
                    n = "qk"[w]
                    if u < 2:
                        pe.wait_ge(s_xTc, b * (2 * TT) + (c + 1) * TPC)
                    if u < 2 * NCH:
                        pe.wait_ge(s_w[n], 16)
                    bank_free(u)
                    for k in range(KC):
                        m = pe.matmul(banks[:, PROJ_BANK + u % PROJ_BANKS, :], w_sb[n][:, k, t * P:(t + 1) * P],
                                      xhT[:, k, c * CH:(c + 1) * CH], start=(k == 0), stop=(k == KC - 1))
                    m.then_inc(s_proj, 1)
                pe.wait_ge(s_w["v"], 16)
                for i in range(TT):
                    u = NSPLIT + i
                    bank_free(u)
                    for k in range(KC):
                        m = pe.matmul(banks[:, PROJ_BANK + u % PROJ_BANKS, :], xhT[:, k, i * P:(i + 1) * P],
                                      w_sb["v"][:, k, :], start=(k == 0), stop=(k == KC - 1))
                    m.then_inc(s_proj, 1)
                pe.wait_ge(s_v, b * TT + TT)

                def unit_scores(n, r, v, free=True):
                    i, j, k0, w, diag = UNITS[v]
                    if free:
                        pe.wait_ge(s_max, n * NU + (v - 1))
                    pe.matmul(banks[:, v % 2, 0:w], qs[0:TERMS, r, j, i * P:(i + 1) * P],
                              ks[0:TERMS, r, j, k0:k0 + w], start=True, stop=True).then_inc(s_sm, 1)

                def scores_T(n, r, s, hp, first):
                    c, kb, w = STEPS[s]
                    q = 2 * s + hp
                    if not (first and q < 2):
                        pe.wait_ge(s_exp, n * ST_PAIRS + (q - 1))
                    for j in range(2 * hp, 2 * hp + 2):
                        m = pe.matmul(banks[:, ST_BANK + 2 * hp + j % 2, 0:w],
                                      ks[0:TERMS + MROWS, r, j, kb * P:(kb + 1) * P],
                                      qs[0:TERMS + MROWS, r, j, (c + 1) * CH - w:(c + 1) * CH], start=True, stop=True)
                    m.then_inc(s_st, 1)

                def pv(n, r, s, first):
                    c, kb, w = STEPS[s]
                    pe.wait_ge(s_exp, n * ST_PAIRS + 2 * (s + 1))
                    if DIAG[s]:
                        pe.wait_ge(s_mask, n * ND + sum(DIAG[:s + 1]))
                    if s == 0:
                        pe.wait_ge(s_vg, n + 1)
                        if not first:
                            pe.wait_ge(s_ot, n * NCH)
                    if s == LAST[0] + 1:
                        pe.wait_ge(s_ot, n * NCH + 1)
                    for j in range(HG):
                        m = pe.matmul(banks[j * SLOT:(j + 1) * SLOT, O_BANK, CH - w:CH], vg[:, r, kb, j, :],
                                      pt[:, s % 2, j, 0:w], start=(kb == 0), stop=(s == LAST[c]))
                    m.then_inc(s_pv, 1)

                def turn_out(n, c):
                    pe.wait_ge(s_ot, n * NCH + (c + 1))
                    for t in range(TPC):
                        m = pe.transpose(banks[:, M_BANK, t * P:(t + 1) * P], oT[:, c, t * P:(t + 1) * P], ident[:, :])
                    m.then_inc(s_oT, 1)

                def turn_max(n):
                    pe.wait_ge(s_mb, n + 1)
                    pe.transpose(misc_b[:, 0:P], mb[:, :], ident_b[:, :]).then_inc(s_mT, 1)

                def stack_ready(n, g, r):
                    q = (r + 1) % BODY
                    each = 16 * STACK_DMAS // BODY
                    pe.wait_ge(s_stack[q], b * (16 * STACK_DMAS * LAPS[q]) + g * each + (1 - q + BODY) * each)

                pe.wait_ge(s_stack[0], b * (16 * STACK_DMAS * LAPS[0]) + 16 * STACK_DMAS)
                for v in range(NU):
                    unit_scores(b * NG, 0, v, v >= 2)
                turn_max(b * NG)

                def group(n, g, r, first, last):
                    pe.wait_ge(s_mrow, n * (16 * MROWS) + 16 * MROWS)
                    for s in range(NS):
                        units = [] if last else list(units_of(s))
                        cuts = [0, (2 * len(units) + 4) // 5, (3 * len(units) + 4) // 5, len(units)]

                        def some_units(x):
                            for v in units[cuts[x]:cuts[x + 1]]:
                                unit_scores(n + 1, (r + 1) % BODY, v)

                        scores_T(n, r, s, 0, first)
                        if s == 0 and not last:
                            stack_ready(n, g, r)
                        some_units(0)
                        scores_T(n, r, s, 1, first)
                        some_units(1)
                        if s:
                            pv(n, r, s - 1, first)
                        some_units(2)
                        if s == OT_PREV_STEP and not first:
                            pe.wait_ge(s_mt, n + 1)
                            turn_out(n - 1, 1)
                        elif s == OT_PREV_STEP:
                            pe.wait_ge(s_mt, n + 1)
                        if s == OT_STEP:
                            if not first:
                                pe.wait_ge(s_on, n * NCH)
                            turn_out(n, 0)
                        if s == MT_STEP and not last:
                            pe.wait_ge(s_on, n * NCH + 1)
                            turn_max(n + 1)
                    pv(n, r, NS - 1, first)

                group_loop(pe, b, group)
                pe.wait_ge(s_on, b * (NG * NCH) + (NG * NCH - 1))
                turn_out(b * NG + (NG - 1), 1)

                pe.wait_ge(s_on, b * (NG * NCH) + NG * NCH)
                pe.wait_ge(s_w["o"], 16)
                pe.wait_ge(s_small, SMALL)
                for i in range(TT + 4):
                    if i < TT:
                        if i >= 2:
                            pe.wait_ge(s_aTc, b * TT + (i - 1))
                        transpose_tile(i % 2, att[:, i, :], s_aT)
                    if 0 <= i - 1 < TT:
                        a = i - 1
                        pe.wait_ge(s_aTc, b * TT + (a + 1))
                        if a >= 2:
                            pe.wait_ge(s_x2, b * TT + (a - 1))
                        for k in range(KC):
                            m = pe.matmul(banks[:, 2 + a % 2, :], attT[:, a % 2, k, :], w_sb["o"][:, k, :],
                                          start=(k == 0), stop=(k == KC - 1))
                        m.then_inc(s_wo, 1)
                    if 0 <= i - 3 < TT:
                        a = i - 3
                        pe.wait_ge(s_xh, b * (2 * TT) + (TT + a + 1))
                        if a >= 2:
                            pe.wait_ge(s_xTc, b * (2 * TT) + (TT + a - 1))
                        transpose_tile(4 + a % 2, xh[:, a % 2, :], s_xT)
                    if 0 <= i - 4 < TT:
                        a = i - 4
                        pe.wait_ge(s_xTc, b * (2 * TT) + (TT + a + 1))
                        if a >= 2:
                            pe.wait_ge(s_hc, b * TT + (a - 1))
                        for k in range(KC):
                            m = pe.matmul(banks[:, 6 + a % 2, 0:ER + E], x2T[:, a % 2, k, :], la_sb[:, k, :],
                                          start=(k == 0), stop=(k == KC - 1))
                        m.then_inc(s_h, 1)
                for q in range(TT // TPC):
                    pe.wait_ge(s_hw, b * TT + (q + 1) * TPC)
                    for t in range(TPC):
                        m = pe.transpose(banks[:, q, t * P:(t + 1) * P], hw[:, q * TPC + t, :], ident[:, :])
                    m.then_inc(s_hT, 1)
                for i in range(TT):
                    if i % TPC == 0:
                        pe.wait_ge(s_hTc, b * (TT // TPC) + (i // TPC + 1))
                    if i >= 4:
                        pe.wait_ge(s_out, b * TT + (i - 3))
                    pe.matmul(banks[:, 2 + i % 4, :], hwT[:, i // TPC, i % TPC, :], lb_sb[:, :],
                              start=True, stop=True).then_inc(s_up, 1)


def kernel(**inputs):
    import numpy as _np
    import concourse.bacc as _bacc
    from concourse import mybir as _mybir
    from concourse.bass_utils import run_bass_kernel_spmd as _run

    f = {n: _np.asarray(a) for n, a in inputs.items()}
    data = {
        "x": f["L0_attn_x"],
        "wq": f["L0_attn_Wq"].T, "bq": f["L0_attn_bq"].reshape(KC, P).T,
        "wk": f["L0_attn_Wk"].T, "bk": f["L0_attn_bk"].reshape(KC, P).T,
        "wv": f["L0_attn_Wv"].T, "bv": f["L0_attn_bv"],
        "wo": f["L0_attn_Wo"].T, "bo": f["L0_attn_bo"],
        "rw": f["L0_ffn_router_w"].T, "rb": f["L0_ffn_router_b"],
        "la": f["L0_ffn_A"].reshape(ER, D).T,
        "lb": f["L0_ffn_Bm"].transpose(0, 2, 1).reshape(ER, D),
    }
    nc = _bacc.Bacc("TRN2", target_bir_lowering=False, num_devices=1)
    arrays, args = {}, []
    for name, a in data.items():
        a = _np.ascontiguousarray(a)
        arrays[f"in_{name}"] = a
        args.append(nc.dram_tensor(f"in_{name}", a.shape, _mybir.dt.from_np(a.dtype), kind="ExternalInput").ap())
    args.append(nc.dram_tensor("out_x", f["L0_attn_x"].shape, F32, kind="ExternalOutput").ap())
    block_kernel(nc, *args)
    r = _run(nc, [arrays], core_ids=[0])
    return r.results[0]["out_x"]
```

```python
from contextlib import ExitStack

import concourse.bass as bass
from concourse import mybir

ALU = mybir.AluOpType
ACT = mybir.ActivationFunctionType
AX = mybir.AxisListType
F32 = mybir.dt.float32
BF16 = mybir.dt.bfloat16

P = 128
BATCH, L, D = 2, 1024, 512
H, HD = 32, 16
E, R, TOP = 8, 16, 2
ER = E * R
LORA_SCALE = 8.0 / R
EPS = 1e-5
Q_SCALE = HD ** -0.5
TT = L // P
KC = D // P
HG = 4
NG = H // HG
CH = 512
NCH = L // CH
TPC = CH // P
SLOT = P // HG
NEG = -1e30
LOW = -3e38

PARTS = 3
Q_PART = (0, 0, 0, 1, 1, 2)
K_PART = (0, 1, 2, 0, 1, 0)
TERMS = HD * len(Q_PART)
MROWS = 2

STEPS = [(c, kb, CH - P * max(0, kb - TPC * c)) for c in range(NCH) for kb in range(TPC * (c + 1))]
NS = len(STEPS)
DIAG = [kb >= TPC * c for c, kb, _ in STEPS]
ND = sum(DIAG)
LAST = [max(s for s in range(NS) if STEPS[s][0] == c) for c in range(NCH)]
UNITS = []
for _i in (0, 7, 1, 6, 2, 5, 3, 4):
    for _j in range(HG):
        for _c in range(_i // TPC):
            UNITS.append((_i, _j, _c * CH, CH, False))
        UNITS.append((_i, _j, (_i // TPC) * CH, P * (_i % TPC + 1), True))
NU = len(UNITS)
DIAG_UNITS = [v for v in range(NU) if UNITS[v][4]]
PV_LAG = 2
NSPLIT = 2 * KC * NCH
STACK_DMAS = 2 * len(Q_PART)
BODY = 3
LOOPS = (NG - 2) // BODY


UNIT_STEPS = 9


def unit_cuts():
    step_cost = [w + 128 for _, _, w in STEPS[:UNIT_STEPS]]
    unit_cost = [u[3] + 128 for u in UNITS]
    cuts, v = [0], 0
    for s in range(UNIT_STEPS):
        while v < NU and sum(unit_cost[:v + 1]) * sum(step_cost) <= sum(unit_cost) * sum(step_cost[:s + 1]):
            v += 1
        cuts.append(v)
    return cuts


CUTS = unit_cuts()
assert CUTS[-1] == NU


def units_of(s):
    return range(CUTS[s], CUTS[s + 1]) if s < UNIT_STEPS else range(0)


LAST_UNIT_STEP = UNIT_STEPS - 1
OT_PREV_STEP, OT_STEP, MT_STEP = PV_LAG, LAST[0] + PV_LAG + 1, LAST_UNIT_STEP + 1

RING = 3


def ring_items(first, last):
    items = []
    for s in range(NS):
        if not last:
            items += [("unit", v) for v in units_of(s)]
        if s == OT_PREV_STEP and not first:
            items.append("out of the group before")
        if s == OT_STEP:
            items.append("out")
        if s == MT_STEP and not last:
            items.append("max rows")
    return items


HEAD_ITEMS = NU + 1
GROUP_ITEMS = len(ring_items(False, False))
MAX_LEFT = GROUP_ITEMS - ring_items(False, False).index("max rows") - 1
assert ring_items(True, False)[-1 - MAX_LEFT] == "max rows"
RING_ROW = HEAD_ITEMS + len(ring_items(True, False)) + (NG - 2) * GROUP_ITEMS + len(ring_items(False, True)) + 1
assert GROUP_ITEMS % RING == 0 and RING_ROW % RING == 0


def ring_base(g, first):
    return HEAD_ITEMS if first else g * GROUP_ITEMS + (HEAD_ITEMS + len(ring_items(True, False)) - GROUP_ITEMS)


def ring_slot(first, at):
    return (ring_base(0, first) + at) % RING


ROUTER_OPS = 22
RT_EXP = 3

ST_PAIRS = 2 * NS
PB = 3
XR = 4
JUNK = 2
PROJ_BANK, PROJ_BANKS = 2, 4
ST_BANK = 2
NPROJ = NSPLIT + TT
LAPS = [len(range(r, NG, BODY)) for r in range(BODY)]
POOL_CONSTS = 9
VEC_CONSTS = 3 + E


FIRST_MAX = NSPLIT // KC + 5


def first_units(u):
    n, k = NPROJ - FIRST_MAX, u - FIRST_MAX
    return range(NU * k // n, NU * (k + 1) // n) if k >= 0 else range(0)


def split_unit(u):
    return u // (2 * NCH), u // NCH % 2, u % NCH


def block_kernel(nc, x, wq, bq, wk, bk, wv, bv, wo, bo, rw, rb, la, lb, out):
    parts = nc.dram_tensor("qk_parts", [BATCH, 2, PARTS, D, L], BF16).ap()
    with ExitStack() as ctx:
        def sb(name, shape, dt=F32):
            return ctx.enter_context(nc.sbuf_tensor(name, shape, dt))

        def sem(name):
            return ctx.enter_context(nc.semaphore(name))

        ident = sb("ident", [P, P])
        ident_b = sb("ident_b", [P, P], BF16)
        strip = sb("strip", [P, CH])
        w_sb = {n: sb(f"w{n}_sb", [P, KC, D]) for n in "qkvo"}
        la_sb = sb("la_sb", [P, KC, ER + E])
        lb_sb = sb("lb_sb", [P, D])
        bias_qk = sb("bias_qk", [P, 2, KC])
        bias_q = sb("bias_q", [P, KC])
        bv_row = sb("bv_row", [P, D])
        bo_row = sb("bo_row", [P, D])
        rb_row = sb("rb_row", [P, E])
        rank = sb("rank", [P, TT, E])
        x_in = sb("x_in", [P, XR, D])
        ln_stat = sb("ln_stat", [P, 2, 6])
        ln_mv = sb("ln_mv", [P, 2, 2])
        ln_var = sb("ln_var", [P, 2])
        ln_rstd = sb("ln_rstd", [P, 2])
        minus_half = sb("minus_half", [P, 1])
        xh = sb("xh", [P, 2, D])
        xhT = sb("xhT", [P, KC, L])
        att = xhT[:, :, :].rearrange("p a b -> p (a b)").rearrange("p (t d) -> p t d", t=TT)
        qf = sb("qf", [P, 2, CH])
        rest = sb("rest", [P, 2, CH])
        split = sb("split", [P, 2, PARTS, CH], BF16)
        v_sb = sb("v_sb", [P, TT, D])
        x2 = v_sb
        vg = sb("vg", [P, BODY, TT, HG, SLOT])
        qs = sb("qs", [P, BODY, HG, L], BF16)
        ks = sb("ks", [P, BODY, HG, L], BF16)
        mx = sb("mx", [P, NCH, HG * TT])
        mf = sb("mf", [P, HG * TT])
        mb = sb("mb", [P, P], BF16)
        mt = sb("mt", [P, P], BF16)
        junk = sb("junk", [P, JUNK, CH], BF16)
        pt = sb("pt", [P, PB, HG, CH])
        oT = sb("oT", [P, NCH, CH])
        rden = sb("rden", [P, 2, HG * TPC])
        attT = sb("attT", [P, 2, KC, P])
        x2T = sb("x2T", [P, 2, KC, P])
        pt_flat = pt[:, :, :, :].rearrange("p a b c -> p (a b c)")
        h_sb = pt_flat[:, 0:TT * (ER + E)].rearrange("p (t n) -> p t n", t=TT)
        hw = pt_flat[:, TT * (ER + E):TT * (2 * ER + E)].rearrange("p (t n) -> p t n", t=TT)
        hwT = sb("hwT", [P, 2, TPC, P])
        rt = sb("rt", [P, 7, TT, E])
        rs = sb("rs", [P, 8, TT])

        banks = ctx.enter_context(nc.psum_tensor("banks", [P, 8, CH], F32))
        O_BANK = 6
        RING_BANKS = (0, 1, 7)

        s_w = {n: sem(f"w_{n}_loaded") for n in "qkvo"}
        s_small = sem("small_loaded")
        s_x = [sem(f"x_loaded{i}") for i in range(XR)]
        s_parts = [sem(f"parts_written{k}") for k in range(4)]
        s_stack = [sem(f"stack_loaded{i}") for i in range(BODY)]
        s_mrow = sem("max_rows_loaded")
        s_y = sem("y_stored")
        s_pool = sem("pool_consts")
        s_vec = sem("vector_consts")
        s_bias = sem("biases_loaded")
        s_bias_q = sem("bias_scaled")
        s_stat = sem("ln_stats")
        s_aggr = sem("ln_aggregated")
        s_var = sem("ln_var_ready")
        s_rstd = sem("ln_rstd_ready")
        s_xh = sem("normed")
        s_xT = sem("normed_transposed")
        s_xTc = sem("normed_T_copied")
        s_proj = sem("projected")
        s_qf = sem("q_copied")
        s_q1 = sem("part1_ready")
        s_r1 = sem("rest_ready")
        s_q2 = sem("part2_ready")
        s_q3 = sem("part3_ready")
        s_v = sem("v_copied")
        s_filled = sem("ring_bank_filled")
        s_emptied = sem("ring_bank_emptied")
        s_neg = sem("minus_one_rows_copied")
        s_mf = sem("row_max")
        s_m1 = sem("row_max_part1")
        s_mb = sem("row_max_parts")
        s_st = sem("scores_T")
        s_exp = sem("probs_T")
        s_mask = sem("probs_masked")
        s_vg = sem("v_group_copied")
        s_pv = sem("pv_done")
        s_ot = sem("out_T_copied")
        s_rd = sem("denominators_inverted")
        s_aT = sem("att_transposed")
        s_aTc = sem("att_T_copied")
        s_xb = sem("x_plus_bias")
        s_wo = sem("att_projected")
        s_x2 = sem("x2_ready")
        s_h = sem("experts_down")
        s_hc = sem("h_copied")
        s_rt = sem("router_step")
        s_re = sem("router_exp")
        s_hw = sem("h_gated")
        s_hT = sem("hw_transposed")
        s_hTc = sem("hw_T_copied")
        s_up = sem("experts_up")
        s_out = sem("y_ready")

        SMALL = 16 * 6

        def group_loop(eng, b, group):
            group(b * NG, 0, 0, True, False)
            with eng.Fori(0, LOOPS) as k:
                for q in range(BODY):
                    g = k * BODY + (1 + q)
                    group(b * NG + g, g, (1 + q) % BODY, False, False)
            group(b * NG + (NG - 1), NG - 1, (NG - 1) % BODY, False, True)

        block = ctx.enter_context(nc.Block())

        @block.sync
        def _(sp):
            with sp.Fori(0, BATCH) as b:
                parts_b = parts[bass.ds(b, 1)]
                x_b, out_b = x[bass.ds(b, 1)], out[bass.ds(b, 1)]
                for i in range(TT):
                    if i >= XR:
                        sp.wait_ge(s_xh, b * (2 * TT) + (i - XR + 1))
                    sp.dma_start(x_in[:, i % XR, :], x_b[0, i * P:(i + 1) * P, :]).then_inc(s_x[i % XR], 16)

                def store_parts(u):
                    t, w, c = split_unit(u)
                    sp.wait_ge(s_q1, b * NSPLIT + u + 1)
                    sp.wait_ge(s_q3, b * NSPLIT + u + 1)
                    dst = parts_b[0, w, :, t * P:(t + 1) * P, c * CH:(c + 1) * CH].rearrange("s d l -> d s l")
                    sp.dma_start(dst, split[:, u % 2, :, :]).then_inc(s_parts[u % 4], 16)

                def load_block(g, r, k):
                    w, n = k // len(Q_PART), k % len(Q_PART)
                    dst, part = ((qs, Q_PART[n]), (ks, K_PART[n]))[w]
                    src = parts_b[0, w, part, bass.ds(g * (HG * HD), HG * HD), :]
                    sp.dma_start(dst[n * HD:(n + 1) * HD, r, :, :],
                                 src.rearrange("(j d) l -> d j l", j=HG)).then_inc(s_stack[r], 16)

                def load_stack(g, r):
                    for k in range(STACK_DMAS):
                        load_block(g, r, k)

                def load_max_rows(g, r):
                    sp.wait_ge(s_emptied, b * RING_ROW + ring_base(g, g == 0))
                    for m in range(MROWS):
                        sp.dma_start(qs[TERMS + m:TERMS + m + 1, r, :, :].rearrange("p j l -> p (j l)"),
                                     mt[m * HG * TT:(m + 1) * HG * TT, :]).then_inc(s_mrow, 16)

                per_unit = BODY * STACK_DMAS // (NSPLIT - NSPLIT // KC)
                blocks = [(g, k) for g in range(BODY) for k in range(STACK_DMAS)]
                for u in range(NSPLIT):
                    store_parts(u)
                    if u < NSPLIT // KC:
                        continue
                    for g, k in blocks[(u - NSPLIT // KC) * per_unit:(u - NSPLIT // KC + 1) * per_unit]:
                        if k == 0:
                            t = g * KC // NG
                            for q in range(4):
                                sp.wait_ge(s_parts[q], b * (16 * NSPLIT // 4) + 16 * (t + 1))
                            sp.nop(nofuse=True)
                        load_block(g, g, k)
                for k in range(4):
                    sp.wait_ge(s_parts[k], b * (16 * NSPLIT // 4) + 16 * KC)
                sp.nop(nofuse=True)
                load_max_rows(0, 0)

                for g in range(NG - BODY):
                    load_max_rows(g + 1, (g + 1) % BODY)
                    sp.wait_ge(s_st, b * (NG * ST_PAIRS) + (g + 1) * ST_PAIRS)
                    load_stack(g + BODY, g % BODY)
                for g in range(NG - BODY + 1, NG):
                    load_max_rows(g, g % BODY)

                for i in range(TT):
                    if i >= XR:
                        sp.wait_ge(s_x2, b * TT + (i - XR + 1))
                    sp.dma_start(x_in[:, i % XR, :], x_b[0, i * P:(i + 1) * P, :]).then_inc(s_x[i % XR], 16)
                for i in range(TT):
                    sp.wait_ge(s_out, b * TT + (i + 1))
                    sp.dma_start(out_b[0, i * P:(i + 1) * P, :], x2[:, i, :]).then_inc(s_y, 16)
            sp.wait_ge(s_y, BATCH * TT * 16)

        @block.gpsimd
        def _(pool):
            pool.memset(ident[:, :], 0.0).then_inc(s_pool, 1)
            pool.memset(ident_b[:, :], 0.0).then_inc(s_pool, 1)
            pool.memset(strip[:, :], 0.0).then_inc(s_pool, 1)
            pool.memset(vg[:, :, :, :, :], 0.0).then_inc(s_pool, 1)
            pool.memset(minus_half[:, :], -0.5).then_inc(s_pool, 1)
            pool.wait_ge(s_pool, 5)
            for m in (ident, ident_b):
                pool.affine_select(out=m[:, :], in_=m[:, :], compare_op=ALU.not_equal, fill=1.0, base=0,
                                   pattern=[[-1, P]], channel_multiplier=1).then_inc(s_pool, 1)
            pool.affine_select(out=strip[:, CH - P:], in_=strip[:, CH - P:], compare_op=ALU.is_ge, fill=NEG, base=0,
                               pattern=[[-1, P]], channel_multiplier=1).then_inc(s_pool, 1)
            pool.memset(vg[:, :, :, :, HD:HD + 1], 1.0).then_inc(s_pool, 1)
            pool.wait_ge(s_pool, POOL_CONSTS)
            pool.wait_ge(s_vec, VEC_CONSTS)
            for i in range(BODY):
                first = 1 if i == 0 else 0
                pool.dma_start(ks[TERMS:TERMS + MROWS, i, first:HG, :],
                               ks[TERMS:TERMS + MROWS, 0, 0, :].unsqueeze(1).to_broadcast([MROWS, HG - first, L])
                               ).then_inc(s_neg, 16)
            with pool.Fori(0, BATCH) as b:
                def copy_v(n, g, r):
                    pool.tensor_copy(vg[:, r, :, :, 0:HD],
                                     v_sb[:, :, bass.ds(g * (HG * HD), HG * HD)].rearrange("p t (j d) -> p t j d", j=HG)
                                     ).then_inc(s_vg, 1)

                def inverse_deviation(m):
                    pool.wait_ge(s_var, b * (2 * TT) + (m + 1))
                    pool.tensor_tensor(out=ln_rstd[:, m % 2:m % 2 + 1], in0=ln_var[:, m % 2:m % 2 + 1],
                                       in1=minus_half[:, :], op=ALU.pow).then_inc(s_rstd, 1)

                for i in range(TT):
                    inverse_deviation(i)
                pool.wait_ge(s_v, b * TT + TT)
                pool.nop(nofuse=True)
                copy_v(b * NG, 0, 0)

                def group(n, g, r, first, last):
                    d = 0
                    for s in range(NS):
                        if DIAG[s]:
                            pool.wait_ge(s_exp, n * ST_PAIRS + 2 * (s + 1))
                            pool.nop(nofuse=True)
                            blk = pt[:, s % PB, :, 0:P]
                            pool.affine_select(out=blk, in_=blk, compare_op=ALU.is_ge, fill=0.0, base=0,
                                               pattern=[[0, HG], [1, P]], channel_multiplier=-1).then_inc(s_mask, 1)
                            d += 1
                        if s == LAST[0] + 1 and not last:
                            copy_v(n + 1, g + 1, (r + 1) % BODY)

                group_loop(pool, b, group)

                for i in range(TT):
                    pool.wait_ge(s_x[i % XR], b * (16 * 2 * TT // XR) + 16 * (TT // XR + i // XR + 1))
                    pool.wait_ge(s_small, SMALL)
                    pool.tensor_tensor(out=x_in[:, i % XR, :], in0=x_in[:, i % XR, :], in1=bo_row[:, :],
                                       op=ALU.add).then_inc(s_xb, 1)
                    if i:
                        inverse_deviation(TT + i - 1)
                inverse_deviation(TT + TT - 1)

        @block.scalar
        def _(act):
            def load_weight(n, w):
                act.dma_start(w_sb[n][:, :, :], w.rearrange("(k p) n -> p k n", p=P)).then_inc(s_w[n], 16)

            act.wait_ge(s_x[XR - 1], 16)
            act.dma_start(bias_qk[:, 0, :], bq).then_inc(s_bias, 16)
            act.dma_start(bias_qk[:, 1, :], bk).then_inc(s_bias, 16)
            load_weight("q", wq)
            load_weight("k", wk)
            for row, src in ((bv_row, bv), (bo_row, bo), (rb_row, rb)):
                n = src.shape[0]
                act.dma_start(row[:, :], src.rearrange("(a n) -> a n", a=1).to_broadcast([P, n])).then_inc(s_small, 16)
            act.dma_start(la_sb[:, :, 0:ER], la.rearrange("(k p) n -> p k n", p=P)).then_inc(s_small, 16)
            act.dma_start(la_sb[:, :, ER:ER + E], rw.rearrange("(k p) n -> p k n", p=P)).then_inc(s_small, 16)
            act.dma_start(lb_sb[:, :], lb).then_inc(s_small, 16)
            load_weight("v", wv)
            load_weight("o", wo)
            with act.Fori(0, BATCH) as b:
                for i in range(TT):
                    act.wait_ge(s_xT, b * (2 * TT) + (i + 1))
                    act.activation(xhT[:, :, i * P:(i + 1) * P], banks[:, i % 2, :].rearrange("p (k c) -> p k c", k=KC),
                                   ACT.Copy).then_inc(s_xTc, 1)
                act.wait_ge(s_bias, 2 * 16)
                act.activation(bias_q[:, :], bias_qk[:, 0, :], ACT.Copy, scale=Q_SCALE).then_inc(s_bias_q, 1)
                act.wait_ge(s_bias_q, b + 1)
                for u in range(NSPLIT):
                    t, w, c = split_unit(u)
                    act.wait_ge(s_proj, b * NPROJ + (u + 1))
                    if u >= 2:
                        act.wait_ge(s_q3, b * NSPLIT + (u - 1))
                        act.wait_ge(s_parts[(u - 2) % 4], b * (16 * NSPLIT // 4) + 16 * ((u - 2) // 4 + 1))
                    src = banks[:, PROJ_BANK + u % PROJ_BANKS, :]
                    bias, scale = (bias_q[:, t:t + 1], Q_SCALE) if w == 0 else (bias_qk[:, 1, t:t + 1], 1.0)
                    act.activation(qf[:, u % 2, :], src, ACT.Identity, bias=bias,
                                   scale=scale).then_inc(s_qf, 1)
                    act.activation(split[:, u % 2, 0, :], src, ACT.Identity, bias=bias,
                                   scale=scale).then_inc(s_q1, 1)

                def copy_out(n, c):
                    act.wait_ge(s_pv, n * NS + (LAST[c] + 1))
                    act.activation(oT[:, c, :], banks[:, O_BANK, :], ACT.Copy).then_inc(s_ot, 1)

                def group(n, g, r, first, last):
                    for s, (c, kb, w) in enumerate(STEPS):
                        for hp in range(2):
                            q = 2 * s + hp
                            act.wait_ge(s_st, n * ST_PAIRS + (q + 1))
                            if not (first and s < PB):
                                act.wait_ge(s_pv, n * NS + (s - PB + 1))
                            act.activation(pt[:, s % PB, 2 * hp:2 * hp + 2, 0:w],
                                           banks[:, ST_BANK + 2 * (q % 2):ST_BANK + 2 * (q % 2) + 2, 0:w],
                                           ACT.Exp).then_inc(s_exp, 1)
                            if hp == 0 and s == PV_LAG - 1 and not first:
                                copy_out(n - 1, 1)
                            if hp == 0 and s == LAST[0] + PV_LAG:
                                copy_out(n, 0)

                group_loop(act, b, group)
                copy_out(b * NG + (NG - 1), 1)

                for i in range(TT + 4):
                    if i < TT:
                        act.wait_ge(s_aT, b * TT + (i + 1))
                        if i >= 2:
                            act.wait_ge(s_wo, b * TT + (i - 1))
                        act.activation(attT[:, i % 2, :, :], banks[:, i % 2, :].rearrange("p (k c) -> p k c", k=KC),
                                       ACT.Copy).then_inc(s_aTc, 1)
                    if 0 <= i - 3 < TT:
                        a = i - 3
                        act.wait_ge(s_xT, b * (2 * TT) + (TT + a + 1))
                        if a >= 2:
                            act.wait_ge(s_h, b * TT + (a - 1))
                        act.activation(x2T[:, a % 2, :, :], banks[:, 4 + a % 2, :].rearrange("p (k c) -> p k c", k=KC),
                                       ACT.Copy).then_inc(s_xTc, 1)
                    if 0 <= i - 4 < TT:
                        a = i - 4
                        act.wait_ge(s_h, b * TT + (a + 1))
                        act.activation(h_sb[:, a, :], banks[:, 6 + a % 2, 0:ER + E], ACT.Copy).then_inc(s_hc, 1)
                act.wait_ge(s_rt, b * ROUTER_OPS + RT_EXP)
                act.activation(rt[:, 2, :, :], rt[:, 1, :, :], ACT.Exp).then_inc(s_re, 1)
                for q in range(TT // TPC):
                    act.wait_ge(s_hT, b * (TT // TPC) + (q + 1))
                    act.activation(hwT[:, q, :, :], banks[:, q, :].rearrange("p (t c) -> p t c", t=TPC),
                                   ACT.Copy).then_inc(s_hTc, 1)

        @block.vector
        def _(dve):
            dve.memset(mx[:, :, :], LOW).then_inc(s_vec, 1)
            dve.memset(mb[:, :], 0.0).then_inc(s_vec, 1)
            dve.memset(ks[TERMS:TERMS + MROWS, 0, 0, :], -1.0).then_inc(s_vec, 1)
            for e in range(E):
                dve.memset(rank[:, :, e:e + 1], float(E - e)).then_inc(s_vec, 1)
            dve.wait_ge(s_vec, VEC_CONSTS)
            dve.wait_ge(s_pool, POOL_CONSTS)

            with dve.Fori(0, BATCH) as b:
                def moments(src, m):
                    k = m % 2
                    dve.bn_stats(ln_stat[:, k, :], src).then_inc(s_stat, 1)
                    dve.wait_ge(s_stat, b * (2 * TT) + (m + 1))
                    dve.nop(nofuse=True)
                    dve.bn_aggr(ln_mv[:, k, :], ln_stat[:, k, :]).then_inc(s_aggr, 1)
                    dve.wait_ge(s_aggr, b * (2 * TT) + (m + 1))
                    dve.tensor_scalar(ln_var[:, k:k + 1], ln_mv[:, k, 1:2], EPS, None, ALU.add).then_inc(s_var, 1)

                def normed(src, i, m):
                    k = m % 2
                    dve.wait_ge(s_rstd, b * (2 * TT) + (m + 1))
                    if i >= 2:
                        dve.wait_ge(s_xT, b * (2 * TT) + (m - 1))
                    dve.tensor_scalar(xh[:, k, :], src, ln_mv[:, k, 0:1], ln_rstd[:, k:k + 1],
                                      ALU.subtract, ALU.mult).then_inc(s_xh, 1)

                for i in range(TT + 1):
                    if i < TT:
                        dve.wait_ge(s_x[i % XR], b * (16 * 2 * TT // XR) + 16 * (i // XR + 1))
                        moments(x_in[:, i % XR, :], i)
                    if i:
                        normed(x_in[:, (i - 1) % XR, :], i - 1, i - 1)

                def filled(k):
                    dve.wait_ge(s_filled, b * RING_ROW + k + 1)

                def unit_max(v, base, at, slot):
                    i, j, k0, w, diag = UNITS[v]
                    dst = mx[:, k0 // CH, j * TT + i:j * TT + i + 1]
                    bank = banks[:, RING_BANKS[slot(at[v])], :]
                    filled(base + at[v])
                    if diag:
                        m = DIAG_UNITS.index(v)
                        if m >= JUNK:
                            dve.wait_ge(s_emptied, b * RING_ROW + base + (at[DIAG_UNITS[m - JUNK]] + 1))
                        dve.nop(nofuse=True)
                        dve.tensor_tensor_reduce(junk[:, m % JUNK, 0:w], bank[:, 0:w], strip[:, CH - w:CH],
                                                 1.0, LOW, ALU.add, ALU.max, dst).then_inc(s_emptied, 1)
                    else:
                        dve.tensor_reduce(dst, bank, AX.X, ALU.max).then_inc(s_emptied, 1)

                def max_parts(n, base, at):
                    dve.wait_ge(s_emptied, b * RING_ROW + base + (at[NU - 1] + 1))
                    dve.tensor_tensor(out=mf[:, :], in0=mx[:, 0, :], in1=mx[:, 1, :], op=ALU.max).then_inc(s_mf, 1)
                    dve.wait_ge(s_mf, n + 1)
                    dve.tensor_copy(mb[:, 0:HG * TT], mf[:, :]).then_inc(s_m1, 1)
                    dve.wait_ge(s_m1, n + 1)
                    dve.tensor_tensor(out=mb[:, HG * TT:2 * HG * TT], in0=mf[:, :], in1=mb[:, 0:HG * TT],
                                      op=ALU.subtract).then_inc(s_mb, 1)

                def copy_max_rows(k, slot):
                    filled(k)
                    dve.tensor_copy(mt[0:MROWS * HG * TT, :],
                                    banks[0:MROWS * HG * TT, RING_BANKS[slot], :].bitcast(BF16)[:, 0:P]).then_inc(s_emptied, 1)

                def normalise(n, g, c, k, slot):
                    src = banks[:, RING_BANKS[slot], :].rearrange("p (t j s) -> p t j s", t=TPC, j=HG)
                    den = rden[:, c, :].rearrange("p (t j) -> p t j", t=TPC)
                    filled(k)
                    dve.reciprocal(den, src[:, :, :, HD]).then_inc(s_rd, 1)
                    dve.wait_ge(s_rd, n * NCH + (c + 1))
                    dst = att[:, c * TPC:(c + 1) * TPC, bass.ds(g * (HG * HD), HG * HD)]
                    dve.tensor_tensor(out=dst.rearrange("p t (j d) -> p t j d", j=HG), in0=src[:, :, :, 0:HD],
                                      in1=den.unsqueeze(3).to_broadcast([P, TPC, HG, HD]), op=ALU.mult).then_inc(s_emptied, 1)

                def split_rest(u):
                    k = u % 2

                    def rest_1():
                        dve.wait_ge(s_qf, b * NSPLIT + (u + 1))
                        dve.wait_ge(s_q1, b * NSPLIT + (u + 1))
                        dve.tensor_tensor(out=rest[:, k, :], in0=qf[:, k, :], in1=split[:, k, 0, :],
                                          op=ALU.subtract).then_inc(s_r1, 1)

                    def part_2():
                        dve.wait_ge(s_r1, b * NSPLIT + (u + 1))
                        dve.tensor_copy(split[:, k, 1, :], rest[:, k, :]).then_inc(s_q2, 1)

                    def part_3():
                        dve.wait_ge(s_q2, b * NSPLIT + (u + 1))
                        dve.tensor_tensor(out=split[:, k, 2, :], in0=rest[:, k, :], in1=split[:, k, 1, :],
                                          op=ALU.subtract).then_inc(s_q3, 1)

                    return [rest_1, part_2, part_3]

                def copy_v(i):
                    def add_bias():
                        if i == 0:
                            dve.wait_ge(s_small, SMALL)
                        dve.wait_ge(s_proj, b * NPROJ + (NSPLIT + i + 1))
                        dve.tensor_tensor(out=v_sb[:, i, :], in0=banks[:, PROJ_BANK + (NSPLIT + i) % PROJ_BANKS, :],
                                          in1=bv_row[:, :], op=ALU.add).then_inc(s_v, 1)

                    return [add_bias]

                own = {v: v for v in range(NU)}
                for u in range(NPROJ + 1):
                    jobs = []
                    if 0 <= u - 1 < NSPLIT:
                        jobs = split_rest(u - 1)
                    elif u - 1 >= NSPLIT:
                        jobs = copy_v(u - 1 - NSPLIT)
                    units = list(first_units(u)) if u < NPROJ else []
                    for k in range(max(len(jobs), len(units))):
                        if k < len(jobs):
                            jobs[k]()
                        if k < len(units):
                            unit_max(units[k], 0, own, lambda at: at % RING)
                max_parts(b * NG, 0, own)
                copy_max_rows(NU, NU % RING)

                def group(n, g, r, first, last):
                    items, base = ring_items(first, last), ring_base(g, first)
                    at = {x[1]: k for k, x in enumerate(items) if x[0] == "unit"}

                    def slot(k):
                        return ring_slot(first, k)

                    for k, x in enumerate(items):
                        if x[0] == "unit":
                            unit_max(x[1], base, at, slot)
                            if x[1] == NU - 1:
                                max_parts(n + 1, base, at)
                        elif x == "max rows":
                            copy_max_rows(base + k, slot(k))
                        elif x == "out":
                            normalise(n, g, 0, base + k, slot(k))
                        else:
                            normalise(n - 1, g - 1, 1, base + k, slot(k))

                group_loop(dve, b, group)
                normalise(b * NG + (NG - 1), NG - 1, 1, RING_ROW - 1, (RING_ROW - 1) % RING)

                for i in range(TT + 1):
                    if i < TT:
                        dve.wait_ge(s_wo, b * TT + (i + 1))
                        dve.wait_ge(s_xb, b * TT + (i + 1))
                        dve.tensor_tensor(out=x2[:, i, :], in0=banks[:, 2 + i % 2, :], in1=x_in[:, i % XR, :],
                                          op=ALU.add).then_inc(s_x2, 1)
                        dve.wait_ge(s_x2, b * TT + (i + 1))
                        moments(x2[:, i, :], TT + i)
                    if i:
                        normed(x2[:, i - 1, :], i - 1, TT + i - 1)

                steps = [0]

                def link(ins):
                    steps[0] += 1
                    ins.then_inc(s_rt, 1)
                    dve.wait_ge(s_rt, b * ROUTER_OPS + steps[0])

                def over_experts(x):
                    return x.unsqueeze(2).to_broadcast([P, TT, E])

                def each(out, a, b_, op):
                    link(dve.tensor_tensor(out=out, in0=a, in1=b_, op=op))

                def row(n):
                    return rs[:, n, :]

                logits, shifted, expd, probs, tmp, first_hot, second_hot = (rt[:, n, :, :] for n in range(7))
                big, z, rz, p1, f1, p2, f2, rg = (row(n) for n in range(8))
                dve.wait_ge(s_hc, b * TT + TT)
                each(logits, h_sb[:, :, ER:ER + E], rb_row[:, :].unsqueeze(1).to_broadcast([P, TT, E]), ALU.add)
                link(dve.tensor_reduce(big, logits, AX.X, ALU.max))
                each(shifted, logits, over_experts(big), ALU.subtract)
                assert steps[0] == RT_EXP
                dve.wait_ge(s_re, b + 1)
                link(dve.tensor_reduce(z, expd, AX.X, ALU.add))
                link(dve.reciprocal(rz, z))
                each(probs, expd, over_experts(rz), ALU.mult)

                def take_best(src, best, mark, hot):
                    link(dve.tensor_reduce(best, src, AX.X, ALU.max))
                    each(tmp, src, over_experts(best), ALU.is_equal)
                    each(tmp, tmp, rank[:, :, :], ALU.mult)
                    link(dve.tensor_reduce(mark, tmp, AX.X, ALU.max))
                    each(hot, tmp, over_experts(mark), ALU.is_equal)

                take_best(probs, p1, f1, first_hot)
                link(dve.scalar_tensor_tensor(out=shifted, in0=first_hot, scalar=-2.0, in1=probs, op0=ALU.mult, op1=ALU.add))
                take_best(shifted, p2, f2, second_hot)
                each(rg, p1, p2, ALU.add)
                link(dve.reciprocal(rg, rg))
                each(tmp, first_hot, second_hot, ALU.add)
                link(dve.scalar_tensor_tensor(out=tmp, in0=tmp, scalar=LORA_SCALE, in1=probs, op0=ALU.mult, op1=ALU.mult))
                each(logits, tmp, over_experts(rg), ALU.mult)
                assert steps[0] == ROUTER_OPS, steps
                for t in range(TT):
                    dve.tensor_tensor(out=hw[:, t, :].rearrange("p (e r) -> p e r", e=E),
                                      in0=h_sb[:, t, 0:ER].rearrange("p (e r) -> p e r", e=E),
                                      in1=logits[:, t, :].unsqueeze(2).to_broadcast([P, E, R]), op=ALU.mult).then_inc(s_hw, 1)
                for i in range(TT):
                    dve.wait_ge(s_up, b * TT + (i + 1))
                    dve.tensor_tensor(out=x2[:, i, :], in0=banks[:, 2 + i % 4, :], in1=x2[:, i, :],
                                      op=ALU.add).then_inc(s_out, 1)

        @block.tensor
        def _(pe):
            pe.wait_ge(s_pool, POOL_CONSTS)
            with pe.Fori(0, BATCH) as b:
                def transpose_tile(bank, src, s):
                    for k in range(KC):
                        m = pe.transpose(banks[:, bank, k * P:(k + 1) * P], src[:, k * P:(k + 1) * P], ident[:, :])
                    m.then_inc(s, 1)

                for i in range(TT):
                    pe.wait_ge(s_xh, b * (2 * TT) + (i + 1))
                    if i >= 2:
                        pe.wait_ge(s_xTc, b * (2 * TT) + (i - 1))
                    transpose_tile(i % 2, xh[:, i % 2, :], s_xT)

                def bank_free(u):
                    v = u - PROJ_BANKS
                    if v >= NSPLIT:
                        pe.wait_ge(s_v, b * TT + (v - NSPLIT + 1))
                    elif v >= 0:
                        pe.wait_ge(s_q1, b * NSPLIT + (v + 1))

                def project(u, between):
                    bank_free(u)
                    bank = banks[:, PROJ_BANK + u % PROJ_BANKS, :]
                    if u < NSPLIT:
                        t, w, c = split_unit(u)
                        n = "qk"[w]
                        if u < 2:
                            pe.wait_ge(s_xTc, b * (2 * TT) + (c + 1) * TPC)
                        if u < 2 * NCH:
                            pe.wait_ge(s_w[n], 16)
                    elif u == NSPLIT:
                        pe.wait_ge(s_w["v"], 16)
                    for k in range(KC):
                        if u < NSPLIT:
                            m = pe.matmul(bank, w_sb[n][:, k, t * P:(t + 1) * P], xhT[:, k, c * CH:(c + 1) * CH],
                                          start=(k == 0), stop=(k == KC - 1))
                        else:
                            i = u - NSPLIT
                            m = pe.matmul(bank, xhT[:, k, i * P:(i + 1) * P], w_sb["v"][:, k, :],
                                          start=(k == 0), stop=(k == KC - 1))
                        if k == KC - 1:
                            m.then_inc(s_proj, 1)
                        for v in between[k::KC]:
                            unit_scores(0, v, v, v % RING, v < RING)

                def emptied(k):
                    pe.wait_ge(s_emptied, b * RING_ROW + k - (RING - 1))

                def unit_scores(r, v, k, slot, fresh=False):
                    i, j, k0, w, diag = UNITS[v]
                    if not fresh:
                        emptied(k)
                    pe.matmul(banks[:, RING_BANKS[slot], 0:w], qs[0:TERMS, r, j, i * P:(i + 1) * P],
                              ks[0:TERMS, r, j, k0:k0 + w], start=True, stop=True).then_inc(s_filled, 1)

                def scores_T(n, r, s, hp, first):
                    c, kb, w = STEPS[s]
                    q = 2 * s + hp
                    if not (first and q < 2):
                        pe.wait_ge(s_exp, n * ST_PAIRS + (q - 1))
                    for j in range(2 * hp, 2 * hp + 2):
                        m = pe.matmul(banks[:, ST_BANK + 2 * hp + j % 2, 0:w],
                                      ks[0:TERMS + MROWS, r, j, kb * P:(kb + 1) * P],
                                      qs[0:TERMS + MROWS, r, j, (c + 1) * CH - w:(c + 1) * CH], start=True, stop=True)
                    m.then_inc(s_st, 1)

                def pv(n, r, s, first):
                    c, kb, w = STEPS[s]
                    pe.wait_ge(s_exp, n * ST_PAIRS + 2 * (s + 1))
                    if DIAG[s]:
                        pe.wait_ge(s_mask, n * ND + sum(DIAG[:s + 1]))
                    if s == 0:
                        pe.wait_ge(s_vg, n + 1)
                        if not first:
                            pe.wait_ge(s_ot, n * NCH)
                    if s == LAST[0] + 1:
                        pe.wait_ge(s_ot, n * NCH + 1)
                    for j in range(HG):
                        m = pe.matmul(banks[j * SLOT:(j + 1) * SLOT, O_BANK, CH - w:CH], vg[:, r, kb, j, :],
                                      pt[:, s % PB, j, 0:w], start=(kb == 0), stop=(s == LAST[c]))
                    m.then_inc(s_pv, 1)

                def turn_out(n, c, k, slot):
                    pe.wait_ge(s_ot, n * NCH + (c + 1))
                    emptied(k)
                    for t in range(TPC):
                        m = pe.transpose(banks[:, RING_BANKS[slot], t * P:(t + 1) * P], oT[:, c, t * P:(t + 1) * P], ident[:, :])
                    m.then_inc(s_filled, 1)

                def turn_max(n, k, slot):
                    pe.wait_ge(s_mb, n + 1)
                    emptied(k)
                    pe.transpose(banks[:, RING_BANKS[slot], :].bitcast(BF16)[:, 0:P], mb[:, :],
                                 ident_b[:, :]).then_inc(s_filled, 1)

                def stack_ready(n, g, r):
                    q = (r + 1) % BODY
                    each = 16 * STACK_DMAS // BODY
                    pe.wait_ge(s_stack[q], b * (16 * STACK_DMAS * LAPS[q]) + g * each + (1 - q + BODY) * each)

                for u in range(NPROJ):
                    if u == FIRST_MAX:
                        pe.wait_ge(s_stack[0], b * (16 * STACK_DMAS * LAPS[0]) + 16 * STACK_DMAS)
                    project(u, list(first_units(u)))
                turn_max(b * NG, NU, NU % RING)
                pe.wait_ge(s_v, b * TT + TT)
                pe.wait_ge(s_neg, 16 * BODY)

                def group(n, g, r, first, last):
                    pe.wait_ge(s_mrow, n * (16 * MROWS) + 16 * MROWS)
                    items, base = ring_items(first, last), ring_base(g, first)
                    for s in range(NS):
                        units = [] if last else list(units_of(s))
                        cuts = [len(units) * x // 4 for x in range(5)]

                        def some_units(a, z):
                            for v in units[cuts[a]:cuts[z]]:
                                k = items.index(("unit", v))
                                unit_scores((r + 1) % BODY, v, base + k, ring_slot(first, k))

                        scores_T(n, r, s, 0, first)
                        if s == 0 and not last:
                            stack_ready(n, g, r)
                        some_units(0, 1)
                        if s >= PV_LAG:
                            pv(n, r, s - PV_LAG, first)
                        elif not first:
                            pv(n - 1, (r - 1) % BODY, NS + s - PV_LAG, False)
                        some_units(1, 2)
                        scores_T(n, r, s, 1, first)
                        some_units(2, 4)
                        if s == OT_PREV_STEP and not first:
                            k = items.index("out of the group before")
                            turn_out(n - 1, 1, base + k, ring_slot(first, k))
                        if s == OT_STEP:
                            k = items.index("out")
                            turn_out(n, 0, base + k, ring_slot(first, k))
                        if s == MT_STEP and not last:
                            k = items.index("max rows")
                            turn_max(n + 1, base + k, ring_slot(first, k))

                group_loop(pe, b, group)
                for s in range(NS - PV_LAG, NS):
                    pv(b * NG + (NG - 1), (NG - 1) % BODY, s, False)
                turn_out(b * NG + (NG - 1), 1, RING_ROW - 1, (RING_ROW - 1) % RING)

                pe.wait_ge(s_emptied, b * RING_ROW + RING_ROW)
                pe.wait_ge(s_w["o"], 16)
                pe.wait_ge(s_small, SMALL)
                for i in range(TT + 4):
                    if i < TT:
                        if i >= 2:
                            pe.wait_ge(s_aTc, b * TT + (i - 1))
                        transpose_tile(i % 2, att[:, i, :], s_aT)
                    if 0 <= i - 1 < TT:
                        a = i - 1
                        pe.wait_ge(s_aTc, b * TT + (a + 1))
                        if a >= 2:
                            pe.wait_ge(s_x2, b * TT + (a - 1))
                        for k in range(KC):
                            m = pe.matmul(banks[:, 2 + a % 2, :], attT[:, a % 2, k, :], w_sb["o"][:, k, :],
                                          start=(k == 0), stop=(k == KC - 1))
                        m.then_inc(s_wo, 1)
                    if 0 <= i - 3 < TT:
                        a = i - 3
                        pe.wait_ge(s_xh, b * (2 * TT) + (TT + a + 1))
                        if a >= 2:
                            pe.wait_ge(s_xTc, b * (2 * TT) + (TT + a - 1))
                        transpose_tile(4 + a % 2, xh[:, a % 2, :], s_xT)
                    if 0 <= i - 4 < TT:
                        a = i - 4
                        pe.wait_ge(s_xTc, b * (2 * TT) + (TT + a + 1))
                        if a >= 2:
                            pe.wait_ge(s_hc, b * TT + (a - 1))
                        for k in range(KC):
                            m = pe.matmul(banks[:, 6 + a % 2, 0:ER + E], x2T[:, a % 2, k, :], la_sb[:, k, :],
                                          start=(k == 0), stop=(k == KC - 1))
                        m.then_inc(s_h, 1)
                for q in range(TT // TPC):
                    pe.wait_ge(s_hw, b * TT + (q + 1) * TPC)
                    for t in range(TPC):
                        m = pe.transpose(banks[:, q, t * P:(t + 1) * P], hw[:, q * TPC + t, :], ident[:, :])
                    m.then_inc(s_hT, 1)
                for i in range(TT):
                    if i % TPC == 0:
                        pe.wait_ge(s_hTc, b * (TT // TPC) + (i // TPC + 1))
                    if i >= 4:
                        pe.wait_ge(s_out, b * TT + (i - 3))
                    pe.matmul(banks[:, 2 + i % 4, :], hwT[:, i // TPC, i % TPC, :], lb_sb[:, :],
                              start=True, stop=True).then_inc(s_up, 1)


def kernel(**inputs):
    import numpy as _np
    import concourse.bacc as _bacc
    from concourse import mybir as _mybir
    from concourse.bass_utils import run_bass_kernel_spmd as _run

    f = {n: _np.asarray(a) for n, a in inputs.items()}
    data = {
        "x": f["L0_attn_x"],
        "wq": f["L0_attn_Wq"].T, "bq": f["L0_attn_bq"].reshape(KC, P).T,
        "wk": f["L0_attn_Wk"].T, "bk": f["L0_attn_bk"].reshape(KC, P).T,
        "wv": f["L0_attn_Wv"].T, "bv": f["L0_attn_bv"],
        "wo": f["L0_attn_Wo"].T, "bo": f["L0_attn_bo"],
        "rw": f["L0_ffn_router_w"].T, "rb": f["L0_ffn_router_b"],
        "la": f["L0_ffn_A"].reshape(ER, D).T,
        "lb": f["L0_ffn_Bm"].transpose(0, 2, 1).reshape(ER, D),
    }
    nc = _bacc.Bacc("TRN2", target_bir_lowering=False, num_devices=1)
    arrays, args = {}, []
    for name, a in data.items():
        a = _np.ascontiguousarray(a)
        arrays[f"in_{name}"] = a
        args.append(nc.dram_tensor(f"in_{name}", a.shape, _mybir.dt.from_np(a.dtype), kind="ExternalInput").ap())
    args.append(nc.dram_tensor("out_x", f["L0_attn_x"].shape, F32, kind="ExternalOutput").ap())
    block_kernel(nc, *args)
    r = _run(nc, [arrays], core_ids=[0])
    return r.results[0]["out_x"]
```

```python
from contextlib import ExitStack

import concourse.bass as bass
from concourse import mybir

ALU = mybir.AluOpType
ACT = mybir.ActivationFunctionType
AX = mybir.AxisListType
F32 = mybir.dt.float32
BF16 = mybir.dt.bfloat16

P = 128
BATCH, L, D = 2, 1024, 512
H, HD = 32, 16
E, R, TOP = 8, 16, 2
ER = E * R
LORA_SCALE = 8.0 / R
EPS = 1e-5
Q_SCALE = HD ** -0.5
TT = L // P
KC = D // P
HG = 4
NG = H // HG
CH = 512
NCH = L // CH
TPC = CH // P
SLOT = P // HG
NEG = -1e30
LOW = -3e38

PARTS = 3
Q_PART = (0, 0, 0, 1, 1, 2)
K_PART = (0, 1, 2, 0, 1, 0)
TERMS = HD * len(Q_PART)
MROWS = 2

STEPS = [(c, kb, CH - P * max(0, kb - TPC * c)) for c in range(NCH) for kb in range(TPC * (c + 1))]
NS = len(STEPS)
DIAG = [kb >= TPC * c for c, kb, _ in STEPS]
ND = sum(DIAG)
LAST = [max(s for s in range(NS) if STEPS[s][0] == c) for c in range(NCH)]
UNITS = []
for _i in (0, 7, 6, 1, 5, 2, 4, 3):
    for _j in range(HG):
        for _c in range(_i // TPC):
            UNITS.append((_i, _j, _c * CH, CH, False))
        UNITS.append((_i, _j, (_i // TPC) * CH, P * (_i % TPC + 1), True))
NU = len(UNITS)
DIAG_UNITS = [v for v in range(NU) if UNITS[v][4]]
PV_LAG = 3
NSPLIT = 2 * KC * NCH
STACK_DMAS = 2 * len(Q_PART)
BODY = 3
LOOPS = (NG - 2) // BODY


UNIT_STEPS = 9
EARLY = 11


def cut(units, steps):
    step_cost = [STEPS[s][2] + P for s in steps]
    unit_cost = [UNITS[v][3] + P for v in units]
    dealt, v = {}, 0
    for x, s in enumerate(steps):
        start = v
        while v < len(units) and sum(unit_cost[:v + 1]) * sum(step_cost) <= sum(unit_cost) * sum(step_cost[:x + 1]):
            v += 1
        dealt[s] = units[start:v]
    assert v == len(units)
    return dealt


DEALT = {**cut(range(EARLY, NU), range(UNIT_STEPS)), **cut(range(EARLY), range(UNIT_STEPS, NS))}


def units_of(s):
    return [("unit" if s < UNIT_STEPS else "early", v) for v in DEALT[s]]


LAST_UNIT_STEP = UNIT_STEPS - 1
OT_PREV_STEP, OT_STEP, MT_STEP = PV_LAG, LAST[0] + PV_LAG + 1, LAST_UNIT_STEP + 1

RING = 3
MT_PLACE = 3


def step_items(s):
    items = units_of(s)
    return items[:MT_PLACE] + ["max rows"] + items[MT_PLACE:] if s == MT_STEP else items


RING_ITEMS = [x for s in range(NS) for x in step_items(s)]
SUMS_BEFORE = {step_items(s + 1)[-1]: s + 1 for s in (OT_PREV_STEP, OT_STEP)}
HEAD_ITEMS = NU + 1 + EARLY
GROUP_ITEMS = len(RING_ITEMS)
RING_ROW = HEAD_ITEMS + (NG - 1) * GROUP_ITEMS
assert GROUP_ITEMS * BODY % RING == 0


def ring_base(g):
    return HEAD_ITEMS + g * GROUP_ITEMS


def ring_slot(r, at):
    return (HEAD_ITEMS + r * GROUP_ITEMS + at) % RING


def pair_items(first):
    items = []
    for s in range(NS):
        items += [("scores", s, 0), ("scores", s, 1)]
        if s == OT_PREV_STEP and not first:
            items.append("out of the group before")
        if s == OT_STEP:
            items.append("out")
    return items


PAIR_GROUP = 2 * NS + NCH
PAIR_ROW = NG * PAIR_GROUP
assert PAIR_GROUP % 2 == 0


def pair_base(g, first):
    return 0 if first else g * PAIR_GROUP - 1


def pair_slot(k, first):
    return (pair_base(1, first) + k) % 2


def unit_places(first):
    if first:
        places = {v: v - EARLY for v in range(EARLY)}
    else:
        places = {v: RING_ITEMS.index(("early", v)) - GROUP_ITEMS for v in range(EARLY)}
    places.update({x[1]: k for k, x in enumerate(RING_ITEMS) if x[0] == "unit"})
    return places


ROUTER_OPS = 21
RT_EXP = 3

PB = 4
XR = 4
JUNK = 2
PROJ_BANK, PROJ_BANKS = 2, 4
ST_BANK = 2
NPROJ = NSPLIT + TT
LAPS = [len(range(r, NG, BODY)) for r in range(BODY)]
POOL_CONSTS = 9
VEC_CONSTS = 3 + E


FIRST_MAX, LAST_MAX = NSPLIT // KC + 5, NPROJ - 5


def head_items(u):
    if FIRST_MAX <= u <= LAST_MAX:
        n, k = LAST_MAX + 1 - FIRST_MAX, u - FIRST_MAX
        return [("unit", v) for v in range(NU * k // n, NU * (k + 1) // n)]
    if u == LAST_MAX + 1:
        return ["max rows"]
    n, k = NPROJ - 2 - LAST_MAX, u - LAST_MAX - 2
    return [("early", v) for v in range(EARLY * k // n, EARLY * (k + 1) // n)] if k >= 0 else []


def split_unit(u):
    return u // (2 * NCH), u % 2, u // 2 % NCH


def tiles_before(u):
    if u == 0:
        return range(0, TPC)
    return range(TPC + 2 * (u - 1), TPC + 2 * u) if u <= 2 else range(0)


def block_kernel(nc, x, wq, bq, wk, bk, wv, bv, wo, bo, rw, rb, la, lb, out):
    parts = nc.dram_tensor("qk_parts", [BATCH, 2, PARTS, D, L], BF16).ap()
    with ExitStack() as ctx:
        def sb(name, shape, dt=F32):
            return ctx.enter_context(nc.sbuf_tensor(name, shape, dt))

        def sem(name):
            return ctx.enter_context(nc.semaphore(name))

        ident = sb("ident", [P, P])
        ident_b = sb("ident_b", [P, P], BF16)
        strip = sb("strip", [P, CH])
        w_sb = {n: sb(f"w{n}_sb", [P, KC, D]) for n in "qkvo"}
        la_sb = sb("la_sb", [P, KC, ER + E])
        lb_sb = sb("lb_sb", [P, D])
        bias_qk = sb("bias_qk", [P, 2, KC])
        bias_q = sb("bias_q", [P, KC])
        bv_row = sb("bv_row", [P, D])
        bo_row = sb("bo_row", [P, D])
        rb_row = sb("rb_row", [P, E])
        rank = sb("rank", [P, TT, E])
        x_in = sb("x_in", [P, XR, D])
        ln_stat = sb("ln_stat", [P, 2, 6])
        ln_mv = sb("ln_mv", [P, 2, 2])
        ln_var = sb("ln_var", [P, 2])
        ln_rstd = sb("ln_rstd", [P, 2])
        minus_half = sb("minus_half", [P, 1])
        xh = sb("xh", [P, 2, D])
        xhT = sb("xhT", [P, KC, L])
        att = xhT[:, :, :].rearrange("p a b -> p (a b)").rearrange("p (t d) -> p t d", t=TT)
        v_sb = sb("v_sb", [P, TT, D])
        x2 = v_sb
        vg = sb("vg", [P, BODY, TT, HG, SLOT])
        qs = sb("qs", [P, BODY, HG, L], BF16)
        ks = sb("ks", [P, BODY, HG, L], BF16)
        mx = sb("mx", [P, BODY, NCH, HG * TT])
        mf = sb("mf", [P, HG * TT])
        mb = sb("mb", [P, P], BF16)
        mt = sb("mt", [P, P], BF16)
        junk = sb("junk", [P, JUNK, CH], BF16)
        pt = sb("pt", [P, PB, HG, CH])
        oT = sb("oT", [P, NCH, CH])
        rden = sb("rden", [P, NCH, HG * TPC])
        turned = sb("turned", [P, NCH, CH])
        x2T = att[:, :, :].rearrange("p t (k c) -> p t k c", k=KC)
        pt_flat = pt[:, :, :, :].rearrange("p a b c -> p (a b c)")
        qf = pt_flat[:, 0:2 * CH].rearrange("p (s c) -> p s c", s=2)
        rest = pt_flat[:, 2 * CH:4 * CH].rearrange("p (s c) -> p s c", s=2)
        split = pt_flat[:, 4 * CH:4 * CH + PARTS * CH].bitcast(BF16).rearrange("p (s n c) -> p s n c", s=2, n=PARTS)
        attT = pt_flat[:, 0:2 * D].rearrange("p (s k c) -> p s k c", s=2, k=KC)
        gx = pt_flat[:, 2 * D:2 * D + TT * ER].rearrange("p (t n) -> p t n", t=TT)
        hwT = pt_flat[:, 2 * D + TT * ER:2 * D + 2 * TT * ER].rearrange("p (s t c) -> p s t c", s=2, t=TPC)
        rt = sb("rt", [P, 7, TT, E])
        rs = sb("rs", [P, 8, TT])

        banks = ctx.enter_context(nc.psum_tensor("banks", [P, 8, CH], F32))
        O_BANK = 6
        LOGIT_BANK, H_BANK = 6, 2
        DOWN_STEP = TT + 1
        RING_BANKS = (0, 1, 7)

        s_w = {n: sem(f"w_{n}_loaded") for n in "qkvo"}
        s_w0 = {n: sem(f"w_{n}_first_tile_loaded") for n in "qk"}
        s_small = sem("small_loaded")
        s_x = [sem(f"x_loaded{i}") for i in range(XR)]
        s_parts = [sem(f"parts_written{k}") for k in range(4)]
        s_stack = [sem(f"stack_loaded{i}") for i in range(BODY)]
        s_mrow = sem("max_rows_loaded")
        s_y = sem("y_stored")
        s_pool = sem("pool_consts")
        s_vec = sem("vector_consts")
        s_bias = sem("biases_loaded")
        s_bias_q = sem("bias_scaled")
        s_stat = sem("ln_stats")
        s_aggr = sem("ln_aggregated")
        s_var = sem("ln_var_ready")
        s_rstd = sem("ln_rstd_ready")
        s_xh = sem("normed")
        s_xT = sem("normed_transposed")
        s_xTc = sem("normed_T_copied")
        s_proj = sem("projected")
        s_qf = sem("q_copied")
        s_q1 = sem("part1_ready")
        s_r1 = sem("rest_ready")
        s_q2 = sem("part2_ready")
        s_q3 = sem("part3_ready")
        s_v = sem("v_copied")
        s_filled = sem("ring_bank_filled")
        s_emptied = sem("ring_bank_emptied")
        s_neg = sem("minus_one_rows_copied")
        s_mf = sem("row_max")
        s_m1 = sem("row_max_part1")
        s_mb = sem("row_max_parts")
        s_pair = sem("pair_filled")
        s_pair_free = sem("pair_emptied")
        s_mask = sem("probs_masked")
        s_vg = sem("v_group_copied")
        s_pv = sem("pv_done")
        s_ot = sem("out_T_copied")
        s_rd = sem("denominators_inverted")
        s_on = sem("out_normalised")
        s_aT = sem("att_transposed")
        s_aTc = sem("att_T_copied")
        s_xb = sem("x_plus_bias")
        s_wo = sem("att_projected")
        s_x2 = sem("x2_ready")
        s_lg = sem("router_logits")
        s_h = sem("experts_down")
        s_hc = sem("h_T_copied")
        s_rt = sem("router_step")
        s_re = sem("router_exp")
        s_gx = sem("gates_expanded")
        s_gT = sem("gates_transposed")
        s_hw = sem("h_T_gated")
        s_up = sem("experts_up")
        s_out = sem("y_ready")

        SMALL = 16 * 6

        def group_loop(eng, b, group):
            group(b * NG, 0, 0, True, False)
            with eng.Fori(0, LOOPS) as k:
                for q in range(BODY):
                    g = k * BODY + (1 + q)
                    group(b * NG + g, g, (1 + q) % BODY, False, False)
            group(b * NG + (NG - 1), NG - 1, (NG - 1) % BODY, False, True)

        block = ctx.enter_context(nc.Block())

        @block.sync
        def _(sp):
            def load_weight(n, w):
                sp.dma_start(w_sb[n][:, :, :], w.rearrange("(k p) n -> p k n", p=P)).then_inc(s_w[n], 16)

            w_view = {n: w.rearrange("(k p) n -> p k n", p=P) for n, w in zip("qk", (wq, wk))}
            sp.wait_ge(s_x[1], 16)
            for n in "qk":
                sp.dma_start(w_sb[n][:, :, 0:P], w_view[n][:, :, 0:P]).then_inc(s_w0[n], 16)
            sp.wait_ge(s_x[XR - 1], 2 * 16)
            for n in "qk":
                sp.dma_start(w_sb[n][:, :, P:], w_view[n][:, :, P:]).then_inc(s_w[n], 16)
            for row, src in ((bv_row, bv), (bo_row, bo), (rb_row, rb)):
                n = src.shape[0]
                sp.dma_start(row[:, :], src.rearrange("(a n) -> a n", a=1).to_broadcast([P, n])).then_inc(s_small, 16)
            sp.dma_start(la_sb[:, :, 0:ER], la.rearrange("(k p) n -> p k n", p=P)).then_inc(s_small, 16)
            sp.dma_start(la_sb[:, :, ER:ER + E], rw.rearrange("(k p) n -> p k n", p=P)).then_inc(s_small, 16)
            sp.dma_start(lb_sb[:, :], lb).then_inc(s_small, 16)
            load_weight("v", wv)
            load_weight("o", wo)
            sp.wait_ge(s_vec, VEC_CONSTS)
            for i in range(BODY):
                first = 1 if i == 0 else 0
                sp.dma_start(ks[TERMS:TERMS + MROWS, i, first:HG, :],
                               ks[TERMS:TERMS + MROWS, 0, 0, :].unsqueeze(1).to_broadcast([MROWS, HG - first, L])
                               ).then_inc(s_neg, 16)
            with sp.Fori(0, BATCH) as b:
                parts_b = parts[bass.ds(b, 1)]
                x_b, out_b = x[bass.ds(b, 1)], out[bass.ds(b, 1)]

                def store_parts(u):
                    t, w, c = split_unit(u)
                    sp.wait_ge(s_q1, b * NSPLIT + u + 1)
                    sp.wait_ge(s_q3, b * NSPLIT + u + 1)
                    dst = parts_b[0, w, :, t * P:(t + 1) * P, c * CH:(c + 1) * CH].rearrange("s d l -> d s l")
                    sp.dma_start(dst, split[:, u % 2, :, :]).then_inc(s_parts[u % 4], 16)

                def load_block(g, r, k):
                    w, n = k // len(Q_PART), k % len(Q_PART)
                    dst, part = ((qs, Q_PART[n]), (ks, K_PART[n]))[w]
                    src = parts_b[0, w, part, bass.ds(g * (HG * HD), HG * HD), :]
                    sp.dma_start(dst[n * HD:(n + 1) * HD, r, :, :],
                                 src.rearrange("(j d) l -> d j l", j=HG)).then_inc(s_stack[r], 16)

                def load_stack(g, r):
                    for k in range(STACK_DMAS):
                        load_block(g, r, k)

                def load_max_rows(g, r):
                    k = ring_base(g - 1) + RING_ITEMS.index("max rows") if g else NU
                    sp.wait_ge(s_emptied, b * RING_ROW + (k + 1))
                    for m in range(MROWS):
                        sp.dma_start(qs[TERMS + m:TERMS + m + 1, r, :, :].rearrange("p j l -> p (j l)"),
                                     mt[m * HG * TT:(m + 1) * HG * TT, :]).then_inc(s_mrow, 16)

                per_unit = 6
                blocks = [(g, k) for g in range(BODY) for k in range(STACK_DMAS)]
                for u in range(NSPLIT):
                    store_parts(u)
                    if u < NSPLIT // KC:
                        continue
                    for g, k in blocks[(u - NSPLIT // KC) * per_unit:(u - NSPLIT // KC + 1) * per_unit]:
                        if k == 0:
                            t = g * KC // NG
                            for q in range(4):
                                sp.wait_ge(s_parts[q], b * (16 * NSPLIT // 4) + 16 * (t + 1))
                            sp.nop(nofuse=True)
                        load_block(g, g, k)
                for k in range(4):
                    sp.wait_ge(s_parts[k], b * (16 * NSPLIT // 4) + 16 * KC)
                sp.nop(nofuse=True)
                load_max_rows(0, 0)

                for g in range(NG - BODY):
                    load_max_rows(g + 1, (g + 1) % BODY)
                    sp.wait_ge(s_pair, b * PAIR_ROW + pair_base(g + 1, False))
                    load_stack(g + BODY, g % BODY)
                for g in range(NG - BODY + 1, NG):
                    load_max_rows(g, g % BODY)

                for i in range(TT):
                    if i >= XR:
                        sp.wait_ge(s_x2, b * TT + (i - XR + 1))
                    sp.dma_start(x_in[:, i % XR, :], x_b[0, i * P:(i + 1) * P, :]).then_inc(s_x[i % XR], 16)
                for i in range(TT):
                    sp.wait_ge(s_out, b * TT + (i + 1))
                    sp.dma_start(out_b[0, i * P:(i + 1) * P, :], x2[:, i, :]).then_inc(s_y, 16)
            sp.wait_ge(s_y, BATCH * TT * 16 + 1)

        @block.gpsimd
        def _(pool):
            pool.memset(ident[:, :], 0.0).then_inc(s_pool, 1)
            pool.memset(ident_b[:, :], 0.0).then_inc(s_pool, 1)
            pool.memset(strip[:, :], 0.0).then_inc(s_pool, 1)
            pool.memset(vg[:, :, :, :, :], 0.0).then_inc(s_pool, 1)
            pool.memset(minus_half[:, :], -0.5).then_inc(s_pool, 1)
            pool.wait_ge(s_pool, 5)
            for m in (ident, ident_b):
                pool.affine_select(out=m[:, :], in_=m[:, :], compare_op=ALU.not_equal, fill=1.0, base=0,
                                   pattern=[[-1, P]], channel_multiplier=1).then_inc(s_pool, 1)
            pool.affine_select(out=strip[:, CH - P:], in_=strip[:, CH - P:], compare_op=ALU.is_ge, fill=NEG, base=0,
                               pattern=[[-1, P]], channel_multiplier=1).then_inc(s_pool, 1)
            pool.memset(vg[:, :, :, :, HD:HD + 1], 1.0).then_inc(s_pool, 1)
            pool.wait_ge(s_pool, POOL_CONSTS)
            with pool.Fori(0, BATCH) as b:
                def copy_v(n, g, r):
                    pool.tensor_copy(vg[:, r, :, :, 0:HD],
                                     v_sb[:, :, bass.ds(g * (HG * HD), HG * HD)].rearrange("p t (j d) -> p t j d", j=HG)
                                     ).then_inc(s_vg, 1)

                def inverse_deviation(m):
                    pool.wait_ge(s_var, b * (2 * TT) + (m + 1))
                    pool.tensor_tensor(out=ln_rstd[:, m % 2:m % 2 + 1], in0=ln_var[:, m % 2:m % 2 + 1],
                                       in1=minus_half[:, :], op=ALU.pow).then_inc(s_rstd, 1)

                for i in range(TT):
                    inverse_deviation(i)
                pool.wait_ge(s_v, b * TT + TT)
                pool.nop(nofuse=True)
                copy_v(b * NG, 0, 0)

                def normalise(n, g, c, k):
                    pool.wait_ge(s_pair_free, b * PAIR_ROW + k + 1)
                    src = turned[:, c, :].rearrange("p (t j s) -> p t j s", t=TPC, j=HG)
                    inverse = rden[:, c, :].rearrange("p (t j) -> p t j", t=TPC)
                    pool.wait_ge(s_rd, n * NCH + (c + 1))
                    dst = att[:, c * TPC:(c + 1) * TPC, bass.ds(g * (HG * HD), HG * HD)]
                    pool.tensor_tensor(out=dst.rearrange("p t (j d) -> p t j d", j=HG), in0=src[:, :, :, 0:HD],
                                       in1=inverse.unsqueeze(3).to_broadcast([P, TPC, HG, HD]),
                                       op=ALU.mult).then_inc(s_on, 1)

                def group(n, g, r, first, last):
                    items, base = pair_items(first), pair_base(g, first)
                    for s in range(NS):
                        if s == OT_PREV_STEP + 1 and not first:
                            normalise(n - 1, g - 1, 1, base + items.index("out of the group before"))
                        if s == OT_STEP + 1:
                            normalise(n, g, 0, base + items.index("out"))
                        if DIAG[s]:
                            pool.wait_ge(s_pair_free, b * PAIR_ROW + base + items.index(("scores", s, 1)) + 1)
                            pool.nop(nofuse=True)
                            blk = pt[:, s % PB, :, 0:P]
                            pool.affine_select(out=blk, in_=blk, compare_op=ALU.is_ge, fill=0.0, base=0,
                                               pattern=[[0, HG], [1, P]], channel_multiplier=-1).then_inc(s_mask, 1)
                        if s == LAST[0] + 1 and not last:
                            copy_v(n + 1, g + 1, (r + 1) % BODY)

                group_loop(pool, b, group)
                normalise(b * NG + (NG - 1), NG - 1, 1, PAIR_ROW - 1)

                for i in range(TT):
                    pool.wait_ge(s_x[i % XR], b * (16 * 2 * TT // XR) + 16 * (TT // XR + i // XR + 1))
                    pool.wait_ge(s_small, SMALL)
                    pool.tensor_tensor(out=x_in[:, i % XR, :], in0=x_in[:, i % XR, :], in1=bo_row[:, :],
                                       op=ALU.add).then_inc(s_xb, 1)
                    if i:
                        inverse_deviation(TT + i - 1)
                inverse_deviation(TT + TT - 1)

        @block.scalar
        def _(act):
            act.dma_start(bias_qk[:, 0, :], bq).then_inc(s_bias, 16)
            act.dma_start(bias_qk[:, 1, :], bk).then_inc(s_bias, 16)
            act.wait_ge(s_bias, 2 * 16)
            act.activation(bias_q[:, :], bias_qk[:, 0, :], ACT.Copy, scale=Q_SCALE).then_inc(s_bias_q, 1)
            act.wait_ge(s_bias_q, 1)
            with act.Fori(0, BATCH) as b:
                def copy_transposed(i):
                    act.wait_ge(s_xT, b * (2 * TT) + (i + 1))
                    act.activation(xhT[:, :, i * P:(i + 1) * P], banks[:, i % 2, :].rearrange("p (k c) -> p k c", k=KC),
                                   ACT.Copy).then_inc(s_xTc, 1)

                x_b = x[bass.ds(b, 1)]

                def load_x(i):
                    if i >= XR:
                        act.wait_ge(s_xh, b * (2 * TT) + (i - XR + 1))
                    act.dma_start(x_in[:, i % XR, :], x_b[0, i * P:(i + 1) * P, :]).then_inc(s_x[i % XR], 16)

                for i in range(XR + 2):
                    load_x(i)
                for i in tiles_before(0):
                    copy_transposed(i)
                    if XR + 2 + i < TT:
                        load_x(XR + 2 + i)
                for u in range(NSPLIT):
                    for i in tiles_before(u + 1):
                        copy_transposed(i)
                    t, w, c = split_unit(u)
                    act.wait_ge(s_proj, b * NPROJ + (u + 1))
                    if u >= 2:
                        act.wait_ge(s_q3, b * NSPLIT + (u - 1))
                        act.wait_ge(s_parts[(u - 2) % 4], b * (16 * NSPLIT // 4) + 16 * ((u - 2) // 4 + 1))
                    src = banks[:, PROJ_BANK + u % PROJ_BANKS, :]
                    bias, scale = (bias_q[:, t:t + 1], Q_SCALE) if w == 0 else (bias_qk[:, 1, t:t + 1], 1.0)
                    act.activation(qf[:, u % 2, :], src, ACT.Identity, bias=bias,
                                   scale=scale).then_inc(s_qf, 1)
                    act.activation(split[:, u % 2, 0, :], src, ACT.Identity, bias=bias,
                                   scale=scale).then_inc(s_q1, 1)

                def copy_out(n, c):
                    act.wait_ge(s_pv, n * NS + (LAST[c] + 1))
                    act.activation(oT[:, c, :], banks[:, O_BANK, :], ACT.Copy).then_inc(s_ot, 1)

                def copy_turned(n, c, k, slot):
                    act.wait_ge(s_pair, b * PAIR_ROW + k + 1)
                    act.activation(turned[:, c, :], banks[:, ST_BANK + 2 * slot, :], ACT.Copy).then_inc(s_pair_free, 1)

                def group(n, g, r, first, last):
                    items, base = pair_items(first), pair_base(g, first)
                    for s, (c, kb, w) in enumerate(STEPS):
                        for hp in range(2):
                            k = items.index(("scores", s, hp))
                            bank = ST_BANK + 2 * pair_slot(k, first)
                            act.wait_ge(s_pair, b * PAIR_ROW + base + k + 1)
                            if not (first and s < PB):
                                act.wait_ge(s_pv, n * NS + (s - PB + 1))
                            act.activation(pt[:, s % PB, 2 * hp:2 * hp + 2, 0:w],
                                           banks[:, bank:bank + 2, 0:w], ACT.Exp).then_inc(s_pair_free, 1)
                            if hp == 0 and s == PV_LAG - 1 and not first:
                                copy_out(n - 1, 1)
                            if hp == 0 and s == LAST[0] + PV_LAG:
                                copy_out(n, 0)
                        if s == OT_PREV_STEP and not first:
                            k = items.index("out of the group before")
                            act.wait_ge(s_on, n * NCH - 1)
                            copy_turned(n - 1, 1, base + k, pair_slot(k, first))
                        if s == OT_STEP:
                            k = items.index("out")
                            if not first:
                                act.wait_ge(s_on, n * NCH - 1)
                            copy_turned(n, 0, base + k, pair_slot(k, first))

                group_loop(act, b, group)
                copy_out(b * NG + (NG - 1), 1)
                act.wait_ge(s_on, b * (NG * NCH) + (NG * NCH - 2))
                copy_turned(b * NG + (NG - 1), 1, PAIR_ROW - 1, (PAIR_ROW - 1) % 2)

                for i in range(TT + 3):
                    if i < TT:
                        act.wait_ge(s_aT, b * TT + (i + 1))
                        if i >= 2:
                            act.wait_ge(s_wo, b * TT + (i - 1))
                        act.activation(attT[:, i % 2, :, :], banks[:, i % 2, :].rearrange("p (k c) -> p k c", k=KC),
                                       ACT.Copy).then_inc(s_aTc, 1)
                    if 0 <= i - 3 < TT:
                        a = i - 3
                        act.wait_ge(s_xT, b * (2 * TT) + (TT + a + 1))
                        act.activation(x2T[:, a, :, :], banks[:, 4 + a % 2, :].rearrange("p (k c) -> p k c", k=KC),
                                       ACT.Copy).then_inc(s_xTc, 1)
                for q in range(TT // TPC):
                    act.wait_ge(s_h, b * (TT // TPC) + (q + 1))
                    act.activation(hwT[:, q, :, :], banks[:, H_BANK + q, :].rearrange("p (t c) -> p t c", t=TPC),
                                   ACT.Copy).then_inc(s_hc, 1)
                    if q == 0:
                        act.wait_ge(s_rt, b * ROUTER_OPS + RT_EXP)
                        act.activation(rt[:, 2, :, :], rt[:, 1, :, :], ACT.Exp).then_inc(s_re, 1)
                act.wait_ge(s_x2, b * TT + TT)

        @block.vector
        def _(dve):
            dve.memset(mx[:, :, :, :], LOW).then_inc(s_vec, 1)
            dve.memset(mb[:, :], 0.0).then_inc(s_vec, 1)
            dve.memset(ks[TERMS:TERMS + MROWS, 0, 0, :], -1.0).then_inc(s_vec, 1)
            for e in range(E):
                dve.memset(rank[:, :, e:e + 1], float(E - e)).then_inc(s_vec, 1)
            dve.nop(nofuse=True).then_inc(s_y, 1)
            dve.wait_ge(s_vec, VEC_CONSTS)
            dve.wait_ge(s_pool, POOL_CONSTS)

            with dve.Fori(0, BATCH) as b:
                def moments(src, m):
                    k = m % 2
                    dve.bn_stats(ln_stat[:, k, :], src).then_inc(s_stat, 1)
                    dve.wait_ge(s_stat, b * (2 * TT) + (m + 1))
                    dve.nop(nofuse=True)
                    dve.bn_aggr(ln_mv[:, k, :], ln_stat[:, k, :]).then_inc(s_aggr, 1)
                    dve.wait_ge(s_aggr, b * (2 * TT) + (m + 1))
                    dve.tensor_scalar(ln_var[:, k:k + 1], ln_mv[:, k, 1:2], EPS, None, ALU.add).then_inc(s_var, 1)

                def normed(src, i, m):
                    k = m % 2
                    dve.wait_ge(s_rstd, b * (2 * TT) + (m + 1))
                    if i >= 2:
                        dve.wait_ge(s_xT, b * (2 * TT) + (m - 1))
                    dve.tensor_scalar(xh[:, k, :], src, ln_mv[:, k, 0:1], ln_rstd[:, k:k + 1],
                                      ALU.subtract, ALU.mult).then_inc(s_xh, 1)

                for i in range(TT + 1):
                    if i < TT:
                        dve.wait_ge(s_x[i % XR], b * (16 * 2 * TT // XR) + 16 * (i // XR + 1))
                        moments(x_in[:, i % XR, :], i)
                    if i:
                        normed(x_in[:, (i - 1) % XR, :], i - 1, i - 1)

                def filled(k):
                    dve.wait_ge(s_filled, b * RING_ROW + k + 1)

                def unit_max(rr, v, base, at, slot):
                    i, j, k0, w, diag = UNITS[v]
                    dst = mx[:, rr, k0 // CH, j * TT + i:j * TT + i + 1]
                    bank = banks[:, RING_BANKS[slot(at[v])], :]
                    filled(base + at[v])
                    if diag:
                        m = DIAG_UNITS.index(v)
                        if m >= JUNK:
                            dve.wait_ge(s_emptied, b * RING_ROW + base + (at[DIAG_UNITS[m - JUNK]] + 1))
                        dve.nop(nofuse=True)
                        dve.tensor_tensor_reduce(junk[:, m % JUNK, 0:w], bank[:, 0:w], strip[:, CH - w:CH],
                                                 1.0, LOW, ALU.add, ALU.max, dst).then_inc(s_emptied, 1)
                    else:
                        dve.tensor_reduce(dst, bank, AX.X, ALU.max).then_inc(s_emptied, 1)

                def max_parts(n, rr, base, at):
                    def row_max():
                        dve.wait_ge(s_emptied, b * RING_ROW + base + (at[NU - 1] + 1))
                        dve.tensor_tensor(out=mf[:, :], in0=mx[:, rr, 0, :], in1=mx[:, rr, 1, :], op=ALU.max).then_inc(s_mf, 1)

                    def part_1():
                        dve.wait_ge(s_mf, n + 1)
                        dve.tensor_copy(mb[:, 0:HG * TT], mf[:, :]).then_inc(s_m1, 1)

                    def part_2():
                        dve.wait_ge(s_m1, n + 1)
                        dve.tensor_tensor(out=mb[:, HG * TT:2 * HG * TT], in0=mf[:, :], in1=mb[:, 0:HG * TT],
                                          op=ALU.subtract).then_inc(s_mb, 1)

                    return [row_max, part_1, part_2]

                def copy_max_rows(k, slot):
                    filled(k)
                    dve.tensor_copy(mt[0:MROWS * HG * TT, :],
                                    banks[0:MROWS * HG * TT, RING_BANKS[slot], :].bitcast(BF16)[:, 0:P]).then_inc(s_emptied, 1)

                def invert_sums(n, c, k):
                    dve.wait_ge(s_pair_free, b * PAIR_ROW + k + 1)
                    dve.reciprocal(rden[:, c, :].rearrange("p (t j) -> p t j", t=TPC),
                                   turned[:, c, :].rearrange("p (t j s) -> p t j s", t=TPC, j=HG)[:, :, :, HD]).then_inc(s_rd, 1)

                def split_rest(u):
                    k = u % 2

                    def rest_1():
                        dve.wait_ge(s_qf, b * NSPLIT + (u + 1))
                        dve.wait_ge(s_q1, b * NSPLIT + (u + 1))
                        dve.tensor_tensor(out=rest[:, k, :], in0=qf[:, k, :], in1=split[:, k, 0, :],
                                          op=ALU.subtract).then_inc(s_r1, 1)

                    def part_2():
                        dve.wait_ge(s_r1, b * NSPLIT + (u + 1))
                        dve.tensor_copy(split[:, k, 1, :], rest[:, k, :]).then_inc(s_q2, 1)

                    def part_3():
                        dve.wait_ge(s_q2, b * NSPLIT + (u + 1))
                        dve.tensor_tensor(out=split[:, k, 2, :], in0=rest[:, k, :], in1=split[:, k, 1, :],
                                          op=ALU.subtract).then_inc(s_q3, 1)

                    return [rest_1, part_2, part_3]

                def copy_v(i):
                    def add_bias():
                        if i == 0:
                            dve.wait_ge(s_small, SMALL)
                            dve.wait_ge(s_y, b * (TT * 16) + 1)
                        dve.wait_ge(s_proj, b * NPROJ + (NSPLIT + i + 1))
                        dve.tensor_tensor(out=v_sb[:, i, :], in0=banks[:, PROJ_BANK + (NSPLIT + i) % PROJ_BANKS, :],
                                          in1=bv_row[:, :], op=ALU.add).then_inc(s_v, 1)

                    return [add_bias]

                own = {v: v for v in range(NU)}
                for u in range(NPROJ + 1):
                    jobs = []
                    if 0 <= u - 1 < NSPLIT:
                        jobs = split_rest(u - 1)
                    elif u - 1 >= NSPLIT:
                        jobs = copy_v(u - 1 - NSPLIT)
                    items = head_items(u) if u < NPROJ else []
                    for k in range(max(len(jobs), len(items))):
                        if k < len(jobs):
                            jobs[k]()
                        if k >= len(items):
                            continue
                        if items[k] == "max rows":
                            copy_max_rows(NU, NU % RING)
                        elif items[k][0] == "unit":
                            unit_max(0, items[k][1], 0, own, lambda at: at % RING)
                            if items[k][1] == NU - 1:
                                for operation in max_parts(b * NG, 0, 0, own):
                                    operation()
                        else:
                            unit_max(1, items[k][1], NU + 1, own, lambda at: (NU + 1 + at) % RING)

                def group(n, g, r, first, last):
                    pairs, pbase = pair_items(first), pair_base(g, first)

                    def sums_of(s):
                        if s == OT_PREV_STEP + 1 and not first:
                            invert_sums(n - 1, 1, pbase + pairs.index("out of the group before"))
                        if s == OT_STEP + 1:
                            invert_sums(n, 0, pbase + pairs.index("out"))

                    if last:
                        for s in range(NS):
                            sums_of(s)
                        return
                    base, places = ring_base(g), unit_places(first)
                    early = {x[1]: k for k, x in enumerate(RING_ITEMS) if x[0] == "early"}

                    def slot(k):
                        return ring_slot(r, k)

                    left = []
                    for k, x in enumerate(RING_ITEMS):
                        if x in SUMS_BEFORE:
                            sums_of(SUMS_BEFORE[x])
                        if x[0] == "unit":
                            unit_max((r + 1) % BODY, x[1], base, places, slot)
                            if x[1] == NU - 1:
                                left = max_parts(n + 1, (r + 1) % BODY, base, places)
                                left.pop(0)()
                        elif x[0] == "early":
                            unit_max((r + 2) % BODY, x[1], base, early, slot)
                            if left:
                                left.pop(0)()
                        else:
                            assert not left
                            copy_max_rows(base + k, slot(k))

                group_loop(dve, b, group)
                invert_sums(b * NG + (NG - 1), 1, PAIR_ROW - 1)

                for i in range(TT + 1):
                    if i < TT:
                        dve.wait_ge(s_wo, b * TT + (i + 1))
                        dve.wait_ge(s_xb, b * TT + (i + 1))
                        dve.tensor_tensor(out=x2[:, i, :], in0=banks[:, 2 + i % 2, :], in1=x_in[:, i % XR, :],
                                          op=ALU.add).then_inc(s_x2, 1)
                        dve.wait_ge(s_x2, b * TT + (i + 1))
                        moments(x2[:, i, :], TT + i)
                    if i:
                        normed(x2[:, i - 1, :], i - 1, TT + i - 1)

                steps = [0]

                def link(ins):
                    steps[0] += 1
                    ins.then_inc(s_rt, 1)
                    dve.wait_ge(s_rt, b * ROUTER_OPS + steps[0])

                def over_experts(x):
                    return x.unsqueeze(2).to_broadcast([P, TT, E])

                def each(out, a, b_, op):
                    link(dve.tensor_tensor(out=out, in0=a, in1=b_, op=op))

                def row(n):
                    return rs[:, n, :]

                logits, shifted, expd, probs, tmp, first_hot, second_hot = (rt[:, n, :, :] for n in range(7))
                big, z, rz, p1, f1, p2, f2, rg = (row(n) for n in range(8))
                dve.wait_ge(s_lg, b * TT + TT)
                each(logits, banks[:, LOGIT_BANK, 0:TT * E].rearrange("p (t e) -> p t e", t=TT), rb_row[:, :].unsqueeze(1).to_broadcast([P, TT, E]), ALU.add)
                link(dve.tensor_reduce(big, logits, AX.X, ALU.max))
                each(shifted, logits, over_experts(big), ALU.subtract)
                assert steps[0] == RT_EXP
                dve.wait_ge(s_re, b + 1)
                link(dve.tensor_reduce(z, expd, AX.X, ALU.add))
                link(dve.reciprocal(rz, z))
                each(probs, expd, over_experts(rz), ALU.mult)

                def take_best(src, best, mark, hot):
                    link(dve.tensor_reduce(best, src, AX.X, ALU.max))
                    each(tmp, src, over_experts(best), ALU.is_equal)
                    each(tmp, tmp, rank[:, :, :], ALU.mult)
                    link(dve.tensor_reduce(mark, tmp, AX.X, ALU.max))
                    each(hot, tmp, over_experts(mark), ALU.is_equal)

                take_best(probs, p1, f1, first_hot)
                link(dve.scalar_tensor_tensor(out=shifted, in0=first_hot, scalar=-2.0, in1=probs, op0=ALU.mult, op1=ALU.add))
                take_best(shifted, p2, f2, second_hot)
                each(rg, p1, p2, ALU.add)
                link(dve.reciprocal(rg, rg))
                each(tmp, first_hot, second_hot, ALU.add)
                link(dve.scalar_tensor_tensor(out=tmp, in0=tmp, scalar=LORA_SCALE, in1=probs, op0=ALU.mult, op1=ALU.mult))
                assert steps[0] == ROUTER_OPS, steps
                for q in range(TT // TPC):
                    tiles = slice(q * TPC, (q + 1) * TPC)
                    dve.tensor_tensor(out=gx[:, tiles, :].rearrange("p t (e r) -> p t e r", e=E),
                                      in0=tmp[:, tiles, :].unsqueeze(3).to_broadcast([P, TPC, E, R]),
                                      in1=rg[:, tiles].unsqueeze(2).unsqueeze(3).to_broadcast([P, TPC, E, R]),
                                      op=ALU.mult).then_inc(s_gx, 1)
                for q in range(TT // TPC):
                    dve.wait_ge(s_gT, b * (TT // TPC) + (q + 1))
                    dve.wait_ge(s_hc, b * (TT // TPC) + (q + 1))
                    dve.tensor_tensor(out=hwT[:, q, :, :], in0=banks[:, q, :].rearrange("p (t c) -> p t c", t=TPC),
                                      in1=hwT[:, q, :, :], op=ALU.mult).then_inc(s_hw, 1)
                for i in range(TT):
                    dve.wait_ge(s_up, b * TT + (i + 1))
                    dve.tensor_tensor(out=x2[:, i, :], in0=banks[:, 2 + i % 4, :], in1=x2[:, i, :],
                                      op=ALU.add).then_inc(s_out, 1)

        @block.tensor
        def _(pe):
            pe.wait_ge(s_pool, POOL_CONSTS)
            with pe.Fori(0, BATCH) as b:
                def transpose_tile(bank, src, s):
                    for k in range(KC):
                        m = pe.transpose(banks[:, bank, k * P:(k + 1) * P], src[:, k * P:(k + 1) * P], ident[:, :])
                    m.then_inc(s, 1)

                def transpose_normed(i):
                    pe.wait_ge(s_xh, b * (2 * TT) + (i + 1))
                    if i >= 2:
                        pe.wait_ge(s_xTc, b * (2 * TT) + (i - 1))
                    transpose_tile(i % 2, xh[:, i % 2, :], s_xT)

                def bank_free(u):
                    v = u - PROJ_BANKS
                    if v >= NSPLIT:
                        pe.wait_ge(s_v, b * TT + (v - NSPLIT + 1))
                    elif v >= 0:
                        pe.wait_ge(s_q1, b * NSPLIT + (v + 1))

                def project(u, between):
                    for i in tiles_before(u):
                        transpose_normed(i)
                    bank_free(u)
                    bank = banks[:, PROJ_BANK + u % PROJ_BANKS, :]
                    if u < NSPLIT:
                        t, w, c = split_unit(u)
                        n = "qk"[w]
                        if u in (0, 2):
                            pe.wait_ge(s_xTc, b * (2 * TT) + (c + 1) * TPC)
                        if u < 2:
                            pe.wait_ge(s_w0[n], 16)
                        elif t == 1 and c == 0:
                            pe.wait_ge(s_w[n], 16)
                    elif u == NSPLIT:
                        pe.wait_ge(s_w["v"], 16)
                    for k in range(KC):
                        if u < NSPLIT:
                            m = pe.matmul(bank, w_sb[n][:, k, t * P:(t + 1) * P], xhT[:, k, c * CH:(c + 1) * CH],
                                          start=(k == 0), stop=(k == KC - 1))
                        else:
                            i = u - NSPLIT
                            m = pe.matmul(bank, xhT[:, k, i * P:(i + 1) * P], w_sb["v"][:, k, :],
                                          start=(k == 0), stop=(k == KC - 1))
                        if k == KC - 1:
                            m.then_inc(s_proj, 1)
                        for x in between[len(between) * k // KC:len(between) * (k + 1) // KC]:
                            if x == "max rows":
                                turn_max(b * NG, NU, NU % RING)
                            elif x[0] == "unit":
                                unit_scores(0, x[1], x[1], x[1] % RING, x[1] < RING)
                            else:
                                unit_scores(1, x[1], NU + 1 + x[1], (NU + 1 + x[1]) % RING)

                def emptied(k):
                    pe.wait_ge(s_emptied, b * RING_ROW + k - (RING - 1))

                def unit_scores(r, v, k, slot, fresh=False):
                    i, j, k0, w, diag = UNITS[v]
                    if not fresh:
                        emptied(k)
                    pe.matmul(banks[:, RING_BANKS[slot], 0:w], qs[0:TERMS, r, j, i * P:(i + 1) * P],
                              ks[0:TERMS, r, j, k0:k0 + w], start=True, stop=True).then_inc(s_filled, 1)

                def pair_free(k):
                    pe.wait_ge(s_pair_free, b * PAIR_ROW + k - 1)

                def scores_T(r, s, hp, g, first):
                    c, kb, w = STEPS[s]
                    k = pair_items(first).index(("scores", s, hp))
                    bank = ST_BANK + 2 * pair_slot(k, first)
                    if first and k == 1:
                        pe.wait_ge(s_v, b * TT + TT)
                    if not (first and k < 2):
                        pair_free(pair_base(g, first) + k)
                    for j in range(2 * hp, 2 * hp + 2):
                        m = pe.matmul(banks[:, bank + j % 2, 0:w], ks[0:TERMS + MROWS, r, j, kb * P:(kb + 1) * P],
                                      qs[0:TERMS + MROWS, r, j, (c + 1) * CH - w:(c + 1) * CH], start=True, stop=True)
                    m.then_inc(s_pair, 1)

                def pv(n, r, s, exps, first):
                    c, kb, w = STEPS[s]
                    pe.wait_ge(s_pair_free, b * PAIR_ROW + exps)
                    if DIAG[s]:
                        pe.wait_ge(s_mask, n * ND + sum(DIAG[:s + 1]))
                    if s == 0:
                        pe.wait_ge(s_vg, n + 1)
                        if not first:
                            pe.wait_ge(s_ot, n * NCH)
                    if s == LAST[0] + 1:
                        pe.wait_ge(s_ot, n * NCH + 1)
                    for j in range(HG):
                        m = pe.matmul(banks[j * SLOT:(j + 1) * SLOT, O_BANK, CH - w:CH], vg[:, r, kb, j, :],
                                      pt[:, s % PB, j, 0:w], start=(kb == 0), stop=(s == LAST[c]))
                    m.then_inc(s_pv, 1)

                def exps_before(s):
                    before = pair_items(False)
                    return before.index(("scores", s, 1)) + 1 - len(before)

                def turn_out(n, c, k, slot):
                    pe.wait_ge(s_ot, n * NCH + (c + 1))
                    pair_free(k)
                    for t in range(TPC):
                        m = pe.transpose(banks[:, ST_BANK + 2 * slot, t * P:(t + 1) * P], oT[:, c, t * P:(t + 1) * P],
                                         ident[:, :])
                    m.then_inc(s_pair, 1)

                def turn_max(n, k, slot):
                    pe.wait_ge(s_mb, n + 1)
                    emptied(k)
                    pe.transpose(banks[:, RING_BANKS[slot], :].bitcast(BF16)[:, 0:P], mb[:, :],
                                 ident_b[:, :]).then_inc(s_filled, 1)

                def stack_ready(g, r):
                    q = (r + 2) % BODY
                    fill = 16 * STACK_DMAS
                    if r == 0 and LAPS[q] == 2:
                        fills = fill if isinstance(g, int) else 2 * fill
                    else:
                        fills = g * (fill // BODY) + (2 - q + BODY) * (fill // BODY)
                    pe.wait_ge(s_stack[q], b * (fill * LAPS[q]) + fills)

                for u in range(NPROJ):
                    if u == FIRST_MAX:
                        pe.wait_ge(s_stack[0], b * (16 * STACK_DMAS * LAPS[0]) + 16 * STACK_DMAS)
                    if u == LAST_MAX + 2:
                        pe.wait_ge(s_stack[1], b * (16 * STACK_DMAS * LAPS[1]) + 16 * STACK_DMAS)
                    project(u, head_items(u))
                pe.wait_ge(s_v, b * TT + (TT - 2))
                pe.wait_ge(s_neg, 16 * BODY)

                def group(n, g, r, first, last):
                    pe.wait_ge(s_mrow, n * (16 * MROWS) + 16 * MROWS)
                    pairs, base = pair_items(first), pair_base(g, first)
                    for s in range(NS):
                        items = [] if last else step_items(s)
                        cuts = [len(items) * x // 4 for x in range(5)]

                        def some_items(a, z):
                            for x in items[cuts[a]:cuts[z]]:
                                k = RING_ITEMS.index(x)
                                if x == "max rows":
                                    turn_max(n + 1, ring_base(g) + k, ring_slot(r, k))
                                else:
                                    ahead = 1 if x[0] == "unit" else 2
                                    unit_scores((r + ahead) % BODY, x[1], ring_base(g) + k, ring_slot(r, k))

                        scores_T(r, s, 0, g, first)
                        if s == UNIT_STEPS and not last:
                            stack_ready(g, r)
                        some_items(0, 1)
                        if s >= PV_LAG:
                            pv(n, r, s - PV_LAG, base + pairs.index(("scores", s - PV_LAG, 1)) + 1, first)
                        elif not first:
                            t = NS + s - PV_LAG
                            pv(n - 1, (r - 1) % BODY, t, base + exps_before(t), False)
                        some_items(1, 2)
                        scores_T(r, s, 1, g, first)
                        some_items(2, 4)
                        if s == OT_PREV_STEP and not first:
                            k = pairs.index("out of the group before")
                            turn_out(n - 1, 1, base + k, pair_slot(k, first))
                        if s == OT_STEP:
                            k = pairs.index("out")
                            turn_out(n, 0, base + k, pair_slot(k, first))

                group_loop(pe, b, group)
                for s in range(NS - PV_LAG, NS):
                    pv(b * NG + (NG - 1), (NG - 1) % BODY, s, PAIR_ROW - 1 + exps_before(s), False)

                pe.wait_ge(s_w["o"], 16)
                pe.wait_ge(s_small, SMALL)
                def down(q):
                    pe.wait_ge(s_x2, b * TT + (TT - 1 + q))
                    for k in range(KC):
                        m = pe.matmul(banks[:, H_BANK + q, :], la_sb[:, k, 0:ER], x2T[:, q * TPC:(q + 1) * TPC, k, :],
                                      start=(k == 0), stop=(k == KC - 1))
                    m.then_inc(s_h, 1)

                for i in range(TT + 4):
                    if i == DOWN_STEP:
                        down(0)
                    if i < TT:
                        if i >= 2:
                            pe.wait_ge(s_aTc, b * TT + (i - 1))
                        if i == 0:
                            pe.wait_ge(s_emptied, b * RING_ROW + RING_ROW)
                            pe.wait_ge(s_on, b * (NG * NCH) + (NG * NCH - 1))
                        if i == TPC:
                            pe.wait_ge(s_on, b * (NG * NCH) + NG * NCH)
                        transpose_tile(i % 2, att[:, i, :], s_aT)
                        if i == 1:
                            turn_out(b * NG + (NG - 1), 1, PAIR_ROW - 1, (PAIR_ROW - 1) % 2)
                    if 0 <= i - 1 < TT:
                        a = i - 1
                        pe.wait_ge(s_aTc, b * TT + (a + 1))
                        if a >= 2:
                            pe.wait_ge(s_x2, b * TT + (a - 1))
                        for k in range(KC):
                            m = pe.matmul(banks[:, 2 + a % 2, :], attT[:, a % 2, k, :], w_sb["o"][:, k, :],
                                          start=(k == 0), stop=(k == KC - 1))
                        m.then_inc(s_wo, 1)
                    if 0 <= i - 3 < TT:
                        a = i - 3
                        pe.wait_ge(s_xh, b * (2 * TT) + (TT + a + 1))
                        if a >= 2:
                            pe.wait_ge(s_xTc, b * (2 * TT) + (TT + a - 1))
                        transpose_tile(4 + a % 2, xh[:, a % 2, :], s_xT)
                    if 0 <= i - 4 < TT:
                        a = i - 4
                        pe.wait_ge(s_xTc, b * (2 * TT) + (TT + a + 1))
                        for k in range(KC):
                            m = pe.matmul(banks[:, LOGIT_BANK, a * E:(a + 1) * E], x2T[:, a, k, :],
                                          la_sb[:, k, ER:ER + E], start=(k == 0), stop=(k == KC - 1))
                        m.then_inc(s_lg, 1)
                down(1)
                for q in range(TT // TPC):
                    pe.wait_ge(s_gx, b * (TT // TPC) + (q + 1))
                    for t in range(TPC):
                        m = pe.transpose(banks[:, q, t * P:(t + 1) * P], gx[:, q * TPC + t, :], ident[:, :])
                    m.then_inc(s_gT, 1)
                pe.wait_ge(s_hc, b * (TT // TPC) + TT // TPC)
                for i in range(TT):
                    if i % TPC == 0:
                        pe.wait_ge(s_hw, b * (TT // TPC) + (i // TPC + 1))
                    if i >= 4:
                        pe.wait_ge(s_out, b * TT + (i - 3))
                    pe.matmul(banks[:, 2 + i % 4, :], hwT[:, i // TPC, i % TPC, :], lb_sb[:, :],
                              start=True, stop=True).then_inc(s_up, 1)


def kernel(**inputs):
    import numpy as _np
    import concourse.bacc as _bacc
    from concourse import mybir as _mybir
    from concourse.bass_utils import run_bass_kernel_spmd as _run

    f = {n: _np.asarray(a) for n, a in inputs.items()}
    data = {
        "x": f["L0_attn_x"],
        "wq": f["L0_attn_Wq"].T, "bq": f["L0_attn_bq"].reshape(KC, P).T,
        "wk": f["L0_attn_Wk"].T, "bk": f["L0_attn_bk"].reshape(KC, P).T,
        "wv": f["L0_attn_Wv"].T, "bv": f["L0_attn_bv"],
        "wo": f["L0_attn_Wo"].T, "bo": f["L0_attn_bo"],
        "rw": f["L0_ffn_router_w"].T, "rb": f["L0_ffn_router_b"],
        "la": f["L0_ffn_A"].reshape(ER, D).T,
        "lb": f["L0_ffn_Bm"].transpose(0, 2, 1).reshape(ER, D),
    }
    nc = _bacc.Bacc("TRN2", target_bir_lowering=False, num_devices=1)
    arrays, args = {}, []
    for name, a in data.items():
        a = _np.ascontiguousarray(a)
        arrays[f"in_{name}"] = a
        args.append(nc.dram_tensor(f"in_{name}", a.shape, _mybir.dt.from_np(a.dtype), kind="ExternalInput").ap())
    args.append(nc.dram_tensor("out_x", f["L0_attn_x"].shape, F32, kind="ExternalOutput").ap())
    block_kernel(nc, *args)
    r = _run(nc, [arrays], core_ids=[0])
    return r.results[0]["out_x"]
```
